# Optimizing a Trainium2 kernel written in Bass

```python
import numpy as np
import jax
import jax.numpy as jnp

def _softmax(x, axis=-1):
    return jax.nn.softmax(x, axis=axis)

def _gelu(x):
    return jax.nn.gelu(x, approximate=True)

def _silu(x):
    return jax.nn.silu(x)

def _sigmoid(x):
    return jax.nn.sigmoid(x)

def _layernorm(x, axis=-1, eps=1e-05):
    m = jnp.mean(x, axis=axis, keepdims=True)
    v = jnp.var(x, axis=axis, keepdims=True)
    return (x - m) / jnp.sqrt(v + eps)

def _scatter_add(tgt, idx, src, axis=0):
    return tgt.at[idx].add(src)

def _segment_sum(src, seg, n):
    return jax.ops.segment_sum(src, seg, n)
kernel_name = 'mk_xattn_ffn_d1_seqx_r2_6a3d5d'

def setup_inputs(seed: int=0):
    np.random.seed(seed)
    _w = jnp.asarray

    def _rec_inputs():
        import jax
        import jax.numpy as jnp
        _rk = jax.random.key(seed)
        x = 7.22e-05 + 1 * jax.random.normal(jax.random.fold_in(_rk, 1), (2, 2048, 512), jnp.float32)
        _lenS = 2048 - jax.random.randint(jax.random.fold_in(_rk, 7), (2,), 0, max(1, 2048 // 4) + 1, jnp.int32)
        _lenS2 = 128 - jax.random.randint(jax.random.fold_in(_rk, 8), (2,), 0, max(1, 128 // 4) + 1, jnp.int32)
        _ctx_1024P = jax.random.normal(jax.random.fold_in(_rk, 11), (2, 16, 512), jnp.float32)
        _ctx_1024c = jax.random.dirichlet(jax.random.fold_in(_rk, 511), 0.3 * jnp.ones((16,), jnp.float32), (2, 128))
        _ctx_1024t = jnp.einsum('bsk,bkd->bsd', _ctx_1024c, _ctx_1024P)
        _ctx_1024t = _ctx_1024t * jax.lax.rsqrt(jnp.mean(jnp.square(_ctx_1024t)) + 1e-12) * 0.953939
        ctx_1024 = -0.000514642 + 1.00011 * (_ctx_1024t + 0.3 * jax.random.normal(jax.random.fold_in(_rk, 611), (2, 128, 512), jnp.float32))
        return (x, ctx_1024)
    x, ctx_1024 = _rec_inputs()

    def _L0_xattn_setup():
        import jax, jax.numpy as jnp
        import numpy as np
        LN_EPS = 1e-05

        def _layernorm(x, gamma, beta):
            mu = jnp.mean(x, axis=-1, keepdims=True)
            var = jnp.mean(jnp.square(x - mu), axis=-1, keepdims=True)
            return (x - mu) * jax.lax.rsqrt(var + LN_EPS) * gamma + beta
        key = jax.random.key(seed)
        ks = jax.random.split(key, 6)
        B, Sq, Skv, D, H = (2, 2048, 512, 512, 16)
        scale = 1.0 / np.sqrt(D)
        return {'hidden_states': jax.random.normal(ks[0], (B, Sq, D), jnp.float32), 'encoder_hidden_states': jax.random.normal(ks[1], (B, Skv, D), jnp.float32), 'Wq': jax.random.normal(ks[2], (D, D), jnp.float32) * scale, 'Wk': jax.random.normal(ks[3], (D, D), jnp.float32) * scale, 'Wv': jax.random.normal(ks[4], (D, D), jnp.float32) * scale, 'Wo': jax.random.normal(ks[5], (D, D), jnp.float32) * scale, 'gq': jnp.ones((D // H,), jnp.float32), 'bq': jnp.zeros((D // H,), jnp.float32), 'gk': jnp.ones((D // H,), jnp.float32), 'bk': jnp.zeros((D // H,), jnp.float32)}
    _L0_xattn_all = _L0_xattn_setup()
    _L0_xattn_in = {k: v for k, v in _L0_xattn_all.items() if k in ('Wq', 'Wk', 'Wv', 'Wo', 'gq', 'bq', 'gk', 'bk')}
    del _L0_xattn_all

    def _L0_ffn_setup():
        import jax, jax.numpy as jnp
        import numpy as np
        D_MODEL = 512
        M = 64
        INNER = 16
        key = jax.random.key(seed)
        ks = jax.random.split(key, 9)

        def init(k, shape, fan_in):
            bound = 1.0 / np.sqrt(fan_in)
            return jax.random.uniform(k, shape, jnp.float32, -bound, bound)
        x = jax.random.normal(ks[0], (16, 2048, D_MODEL), dtype=jnp.float32)
        Win = init(ks[1], (D_MODEL, M), D_MODEL)
        bin_ = init(ks[2], (M,), D_MODEL)
        W1 = init(ks[3], (M, INNER), 1)
        b1 = init(ks[4], (M, INNER), 1)
        W2 = init(ks[5], (M, INNER), INNER)
        b2 = init(ks[6], (M,), INNER)
        Wout = init(ks[7], (M, D_MODEL), M)
        bout = init(ks[8], (D_MODEL,), M)
        return {'x': x, 'Win': Win, 'bin_': bin_, 'W1': W1, 'b1': b1, 'W2': W2, 'b2': b2, 'Wout': Wout, 'bout': bout}
    _L0_ffn_all = _L0_ffn_setup()
    _L0_ffn_in = {k: v for k, v in _L0_ffn_all.items() if k in ('Win', 'bin_', 'W1', 'b1', 'W2', 'b2', 'Wout', 'bout')}
    del _L0_ffn_all
    return {'x': x, 'ctx_1024': ctx_1024, 'L0_xattn_Wq': _L0_xattn_in['Wq'], 'L0_xattn_Wk': _L0_xattn_in['Wk'], 'L0_xattn_Wv': _L0_xattn_in['Wv'], 'L0_xattn_Wo': _L0_xattn_in['Wo'], 'L0_xattn_gq': _L0_xattn_in['gq'], 'L0_xattn_bq': _L0_xattn_in['bq'], 'L0_xattn_gk': _L0_xattn_in['gk'], 'L0_xattn_bk': _L0_xattn_in['bk'], 'L0_ffn_Win': _L0_ffn_in['Win'], 'L0_ffn_bin_': _L0_ffn_in['bin_'], 'L0_ffn_W1': _L0_ffn_in['W1'], 'L0_ffn_b1': _L0_ffn_in['b1'], 'L0_ffn_W2': _L0_ffn_in['W2'], 'L0_ffn_b2': _L0_ffn_in['b2'], 'L0_ffn_Wout': _L0_ffn_in['Wout'], 'L0_ffn_bout': _L0_ffn_in['bout']}

def reference(x, ctx_1024, L0_xattn_Wq, L0_xattn_Wk, L0_xattn_Wv, L0_xattn_Wo, L0_xattn_gq, L0_xattn_bq, L0_xattn_gk, L0_xattn_bk, L0_ffn_Win, L0_ffn_bin_, L0_ffn_W1, L0_ffn_b1, L0_ffn_W2, L0_ffn_b2, L0_ffn_Wout, L0_ffn_bout):
    import jax
    import jax.numpy as jnp

    def _L0_xattn_ref(hidden_states, encoder_hidden_states, Wq, Wk, Wv, Wo, gq, bq, gk, bk):
        import jax, jax.numpy as jnp
        import numpy as np
        LN_EPS = 1e-05

        def _layernorm(x, gamma, beta):
            mu = jnp.mean(x, axis=-1, keepdims=True)
            var = jnp.mean(jnp.square(x - mu), axis=-1, keepdims=True)
            return (x - mu) * jax.lax.rsqrt(var + LN_EPS) * gamma + beta
        H = 16
        B, Sq, D = hidden_states.shape
        Skv = encoder_hidden_states.shape[1]
        hd = D // H
        q = hidden_states @ Wq
        k = encoder_hidden_states @ Wk
        v = encoder_hidden_states @ Wv
        q = q.reshape(B, Sq, H, hd).transpose(0, 2, 1, 3)
        k = k.reshape(B, Skv, H, hd).transpose(0, 2, 1, 3)
        v = v.reshape(B, Skv, H, hd).transpose(0, 2, 1, 3)
        q = _layernorm(q, gq, bq)
        k = _layernorm(k, gk, bk)
        scale = 1.0 / np.sqrt(hd).astype(np.float32)
        scores = jnp.einsum('bhqd,bhkd->bhqk', q, k) * scale
        attn = jax.nn.softmax(scores, axis=-1)
        out = jnp.einsum('bhqk,bhkd->bhqd', attn, v)
        out = out.transpose(0, 2, 1, 3).reshape(B, Sq, D)
        return out @ Wo

    def _L0_ffn_ref(x, Win, bin_, W1, b1, W2, b2, Wout, bout):
        import jax, jax.numpy as jnp
        import numpy as np
        D_MODEL = 512
        M = 64
        INNER = 16
        s = jnp.einsum('btd,dm->btm', x, Win) + bin_
        h = jax.nn.relu(s[..., None] * W1 + b1)
        g = jnp.einsum('btmh,mh->btm', h, W2) + b2
        out = jnp.einsum('btm,md->btd', g, Wout) + bout
        return out
    x = x + _L0_xattn_ref(_layernorm(x, axis=-1), ctx_1024, L0_xattn_Wq, L0_xattn_Wk, L0_xattn_Wv, L0_xattn_Wo, L0_xattn_gq, L0_xattn_bq, L0_xattn_gk, L0_xattn_bk)
    x = x + _L0_ffn_ref(_layernorm(x, axis=-1), L0_ffn_Win, L0_ffn_bin_, L0_ffn_W1, L0_ffn_b1, L0_ffn_W2, L0_ffn_b2, L0_ffn_Wout, L0_ffn_bout)
    return x

_drawn_inputs = setup_inputs


def setup_inputs(seed=0):
    import zlib

    import numpy as np

    out = dict(_drawn_inputs(seed))
    spreads = {'L0_xattn_gq': (1.0, 0.2),
     'L0_xattn_bq': (0.0, 0.516),
     'L0_xattn_gk': (1.0, 0.2),
     'L0_xattn_bk': (0.0, 2.0)}
    factors = {'L0_ffn_bin_': 21.546}
    for name, (base, spread) in spreads.items():
        noise = np.random.default_rng([zlib.crc32(name.encode()), seed]).standard_normal(out[name].shape)
        drawn = base * np.exp(spread * noise) if base else spread * noise
        out[name] = jnp.asarray(drawn.astype(out[name].dtype))
    for name, factor in factors.items():
        out[name] = (out[name] * factor).astype(out[name].dtype)
    return out
```

```python
import concourse.bass as bass
from concourse import mybir
from contextlib import ExitStack

F32 = mybir.dt.float32
F32R = mybir.dt.float32r
ALU = mybir.AluOpType
ACT = mybir.ActivationFunctionType
AX = mybir.AxisListType

P = 128
D = 512
C = D // P
H = 16
HD = D // H
HC = H // C
NB = 2
SQ = 2048
KV = 128
TB = 4
TOK = TB * P
BLOCKS = NB * SQ // TOK
M = 64
INNER = 16
HH = INNER // 2
EPS = 1e-5
SCALE = HD ** -0.5
PR = 4
RR = 4


def build_program(nc, x, ctx_kv, Wq, Wk, Wv, Wo, gq, bq, gk, bk, Win, bin_, W1, b1, W2, b2, Wout, bout, out):
    with ExitStack() as stack:
        def sb(name, shape, dt=F32):
            return stack.enter_context(nc.sbuf_tensor(name, shape, dt))

        def bank(name):
            return stack.enter_context(nc.psum_tensor(name, [P, D], F32))

        def sem(name):
            return stack.enter_context(nc.semaphore(name))

        wq_hi = sb("wq_hi", [P, C, D], F32R)
        wq_lo = sb("wq_lo", [P, C, D], F32R)
        wo_hi = sb("wo_hi", [P, C, D], F32R)
        wo_lo = sb("wo_lo", [P, C, D], F32R)
        win_hi = sb("win_hi", [P, C, 2, M], F32R)
        win_lo = sb("win_lo", [P, C, 2, M], F32R)
        wout2 = sb("wout2", [P, D])
        w2_diag = sb("w2_diag", [P, HH, M])
        bout_row = sb("bout_row", [P, D])
        k_hi = [sb(f"k_hi{b}", [P, C, HC, KV], F32R) for b in range(NB)]
        k_lo = [sb(f"k_lo{b}", [P, C, HC, KV], F32R) for b in range(NB)]
        v_kv = [sb(f"v_kv{b}", [P, D]) for b in range(NB)]
        gq_col = sb("gq_col", [P, 1])
        bq_col = sb("bq_col", [P, 1])
        gk_row = sb("gk_row", [P, HD])
        bk_row = sb("bk_row", [P, HD])
        bin_col = sb("bin_col", [P, 1])
        w1_col = sb("w1_col", [P, HH])
        b1_col = sb("b1_col", [P, HH])
        w2_col = sb("w2_col", [P, HH])
        b2_col = sb("b2_col", [P, 1])
        ident = sb("ident", [P, P])
        neg_ident = sb("neg_ident", [P, P], F32R)
        den_sel = sb("den_sel", [P, C, HD])
        bc_sel = sb("bc_sel", [P, C, P], F32R)
        xin = sb("xin", [P, TB, D])
        zt_hi = sb("zt_hi", [P, 2, C, P], F32R)
        zt_lo = sb("zt_lo", [P, 2, C, P], F32R)
        u = sb("u", [P, TB, D])
        sq = sb("sq", [P, D])
        qt_hi = sb("qt_hi", [P, C, TOK], F32R)
        qt_lo = sb("qt_lo", [P, C, TOK], F32R)
        mx = sb("mx", [P, TB, P])
        mxt = sb("mxt", [P, TOK], F32R)
        prob = sb("prob", [P, PR, TOK])
        att = sb("att", [P, C, TOK])
        at_hi = sb("at_hi", [P, C, TOK], F32R)
        at_lo = sb("at_lo", [P, C, TOK], F32R)
        rden = sb("rden", [P, TOK])
        bc_sel_f = rden[:, :].rearrange("p (c n) -> p c n", c=C)
        rden_hi = sb("rden_hi", [P, TOK], F32R)
        rden_lo = sb("rden_lo", [P, TOK], F32R)
        x1 = sb("x1", [P, TB, D])
        z2 = sb("z2", [P, 2, D])
        z2t_hi = sb("z2t_hi", [P, C, TOK], F32R)
        z2t_lo = sb("z2t_lo", [P, C, TOK], F32R)
        s_in = sb("s_in", [P, TOK])
        pair_eye = s_in[:, 0:M]
        hid = sb("hid", [P, RR, TOK])
        g = sb("g", [P, TOK])
        bn1 = sb("bn1", [P, TB, 6])
        mv1 = sb("mv1", [P, TB, 2])
        bn2 = sb("bn2", [P, TB, 6])
        mv2 = sb("mv2", [P, TB, 2])
        ssq = sb("ssq", [P, TB, H])
        ln1 = sb("ln1", [P, 4, TB])
        ln2 = sb("ln2", [P, 4, TB])
        spare = sb("spare", [P, 1])
        lnq = sb("lnq", [P, 4, TB * H])

        S = [bank("S0"), bank("S1")]
        AT = bank("AT")
        DEN = bank("DEN")
        TR = [bank("TR0"), bank("TR1")]
        PJ = [bank("PJ0"), bank("PJ1")]

        params_loaded = sem("params_loaded")
        wq_loaded = sem("wq_loaded")
        wo_loaded = sem("wo_loaded")
        kvin_loaded = sem("kvin_loaded")
        consts = sem("consts")
        eyes = sem("eyes")
        setup_pe = sem("setup_pe")
        setup_act = sem("setup_act")
        setup_dve = sem("setup_dve")
        setup_done = sem("setup_done")
        x_loaded = [sem(f"x_loaded{j}") for j in range(TB)]
        xr_loaded = [sem(f"xr_loaded{j}") for j in range(TB)]
        stored = [sem(f"stored{j}") for j in range(TB)]
        bn1_done = sem("bn1_done")
        mv1_done = sem("mv1_done")
        ln1_act = sem("ln1_act")
        ln1_step = sem("ln1_step")
        z1_done = sem("z1_done")
        z1_turned = sem("z1_turned")
        zt_hi_done = sem("zt_hi_done")
        zt_lo_done = sem("zt_lo_done")
        q_done = sem("q_done")
        u_done = sem("u_done")
        sq_done = sem("sq_done")
        ssq_done = sem("ssq_done")
        lnq_act = sem("lnq_act")
        lnq_step = sem("lnq_step")
        un_done = sem("un_done")
        q_turned = sem("q_turned")
        qt_hi_done = sem("qt_hi_done")
        qf_done = sem("qf_done")
        qt_lo_done = sem("qt_lo_done")
        maxs_done = sem("maxs_done")
        mx_done = sem("mx_done")
        mx_turned = sem("mx_turned")
        mxt_done = sem("mxt_done")
        scores_done = sem("scores_done")
        exp_done = sem("exp_done")
        pv_done = sem("pv_done")
        att_moved = sem("att_moved")
        rden_done = sem("rden_done")
        rden_hi_done = sem("rden_hi_done")
        rden_lo_done = sem("rden_lo_done")
        spread_done = sem("spread_done")
        att_done = sem("att_done")
        at_hi_done = sem("at_hi_done")
        at_lo_done = sem("at_lo_done")
        o_done = sem("o_done")
        x1_done = sem("x1_done")
        bn2_done = sem("bn2_done")
        mv2_done = sem("mv2_done")
        ln2_act = sem("ln2_act")
        ln2_step = sem("ln2_step")
        z2_done = sem("z2_done")
        bout_added = sem("bout_added")
        z2_turned = sem("z2_turned")
        z2t_hi_done = sem("z2t_hi_done")
        z2t_lo_done = sem("z2t_lo_done")
        s_mm_done = sem("s_mm_done")
        s_done = sem("s_done")
        hid_done = sem("hid_done")
        hsum_done = sem("hsum_done")
        g_done = sem("g_done")
        y_done = sem("y_done")
        out_done = sem("out_done")

        block = stack.enter_context(nc.Block())

        x_t = x.rearrange("b (n j p) d -> (b n) j p d", p=P, j=TB)
        out_t = out.rearrange("b (n j p) d -> (b n) j p d", p=P, j=TB)

        def iterations(engine, iteration):
            per = BLOCKS // NB
            iteration(-1, 0, 0, True, False, False)
            iteration(0, 0, 0, True, True, False)
            with engine.Fori(1, per - 1) as t:
                iteration(t, 0, 0, True, True, True)
            iteration(per - 1, 0, 1, True, True, True)
            with engine.Fori(per, BLOCKS - 1) as t:
                iteration(t, 1, 1, True, True, True)
            iteration(BLOCKS - 1, 1, 1, False, True, True)
            iteration(BLOCKS, 1, 1, False, False, True)

        def first(t):
            return isinstance(t, int) and t <= 0

        @block.sync
        def _(sp):
            sp.dma_start(att[:, :, :], Wk.rearrange("(c p) n -> p c n", p=P)).then_inc(kvin_loaded, 16)
            sp.dma_start(prob[:, 0:NB, :], ctx_kv.rearrange("b k d -> k b d")).then_inc(kvin_loaded, 16)
            sp.dma_start(u[:, :, :], Wv.rearrange("(c p) n -> p c n", p=P)).then_inc(kvin_loaded, 16)
            sp.dma_start(x1[:, :, :], Wq.rearrange("(c p) n -> p c n", p=P)).then_inc(wq_loaded, 16)
            sp.dma_start(xin[:, :, :], Wo.rearrange("(c p) n -> p c n", p=P)).then_inc(wo_loaded, 16)
            sp.dma_start(z2[:, 0, 0:C * M].rearrange("p (c m) -> p c m", c=C),
                         Win.rearrange("(c p) m -> p c m", p=P)).then_inc(wo_loaded, 16)
            sp.wait_ge(setup_done, 1)

            def load_x(T, j):
                if not first(T):
                    sp.wait_ge(z1_turned, T * TB + j + 1 - TB)
                sp.dma_start(xin[:, j, :], x_t[T, j]).then_inc(x_loaded[j], 16)

            def load_residual(T, j):
                if not first(T):
                    sp.wait_ge(stored[j], T * 16)
                sp.dma_start(x1[:, j, :], x_t[T, j]).then_inc(xr_loaded[j], 16)

            def iteration(t, has_f, has_a, has_b):
                if has_b:
                    for j in range(TB):
                        sp.wait_ge(out_done, (t - 1) * TB + j + 1)
                        sp.dma_start(out_t[t - 1, j], x1[:, j, :]).then_inc(stored[j], 16)
                if has_a:
                    for j in range(TB):
                        load_residual(t, j)
                if has_f:
                    for j in range(TB):
                        load_x(t + 2, j)

            for j in range(TB):
                load_x(0, j)
            iteration(-1, True, False, False)
            iteration(0, True, True, False)
            with sp.Fori(1, BLOCKS - 2) as t:
                iteration(t, True, True, True)
            iteration(BLOCKS - 2, False, True, True)
            iteration(BLOCKS - 1, False, True, True)
            iteration(BLOCKS, False, False, True)
            for j in range(TB):
                sp.wait_ge(stored[j], BLOCKS * 16)

        @block.gpsimd
        def _(pool):
            pool.memset(ident[:, :], 0.0).then_inc(eyes, 1)
            pool.memset(bc_sel_f[:, :, :], 0.0).then_inc(eyes, 1)
            pool.memset(den_sel[:, :, :], 0.0).then_inc(eyes, 1)
            pool.memset(mx[:, :, :], 0.0).then_inc(eyes, 1)
            pool.memset(b2_col[:, :], 0.0).then_inc(eyes, 1)
            for b in range(NB):
                pool.memset(k_hi[b][:, :, :, :].bitcast(F32), 0.0).then_inc(eyes, 1)
                pool.memset(k_lo[b][:, :, :, :].bitcast(F32), 0.0).then_inc(eyes, 1)
            pool.wait_ge(eyes, 5 + 2 * NB)
            pool.affine_select(out=ident[:, :], in_=ident[:, :], compare_op=ALU.not_equal, fill=1.0,
                               base=0, pattern=[[-1, P]], channel_multiplier=1).then_inc(consts, 1)
            sel = bc_sel_f[:, :, :].rearrange("p c (i d) -> p c i d", i=HC)
            pool.affine_select(out=sel, in_=sel, compare_op=ALU.not_equal, fill=1.0, base=0,
                               pattern=[[-8, C], [-HD, HC], [0, HD]], channel_multiplier=1).then_inc(consts, 1)
            for c in range(C):
                pool.memset(den_sel[:, c, 8 * c:8 * c + 8], 1.0).then_inc(consts, 1)
            for i in range(HC):
                rows = slice(HD * i, HD * (i + 1))
                pool.dma_start(gq_col[rows, :], gq.rearrange("(p o) -> p o", o=1)).then_inc(params_loaded, 16)
                pool.dma_start(bq_col[rows, :], bq.rearrange("(p o) -> p o", o=1)).then_inc(params_loaded, 16)
            pool.dma_start(gk_row[:, :], gk.rearrange("(o n) -> o n", o=1).broadcast_to([P, HD])).then_inc(params_loaded, 16)
            pool.dma_start(bk_row[:, :], bk.rearrange("(o n) -> o n", o=1).broadcast_to([P, HD])).then_inc(params_loaded, 16)
            pool.dma_start(bout_row[:, :], bout.rearrange("(o n) -> o n", o=1).broadcast_to([P, D])).then_inc(params_loaded, 16)
            pool.dma_start(b2_col[0:M, :], b2.rearrange("(p o) -> p o", o=1)).then_inc(params_loaded, 16)
            for half in range(2):
                rows, units = slice(M * half, M * (half + 1)), slice(HH * half, HH * (half + 1))
                pool.dma_start(bin_col[rows, :], bin_.rearrange("(p o) -> p o", o=1)).then_inc(params_loaded, 16)
                pool.dma_start(w1_col[rows, :], W1[:, units]).then_inc(params_loaded, 16)
                pool.dma_start(b1_col[rows, :], b1[:, units]).then_inc(params_loaded, 16)
                pool.dma_start(w2_col[rows, :], W2[:, units]).then_inc(params_loaded, 16)
                pool.dma_start(wout2[rows, :], Wout).then_inc(params_loaded, 16)

            def square(T, j):
                pool.wait_ge(u_done, T * TB + j + 1)
                if not (first(T) and j == 0):
                    pool.wait_ge(ssq_done, T * TB + j)
                pool.tensor_tensor(sq[:, :], u[:, j, :], u[:, j, :], ALU.mult).then_inc(sq_done, 1)

            def q_low(T, j):
                cols = slice(j * P, (j + 1) * P)
                pool.wait_ge(qf_done, T * TB + j + 1)
                pool.wait_ge(qt_hi_done, T * TB + j + 1)
                pool.tensor_tensor(qt_lo[:, :, cols], u[:, j, :].rearrange("p (c n) -> p c n", c=C),
                                   qt_hi[:, :, cols].bitcast(F32), ALU.subtract).then_inc(qt_lo_done, 1)

            def att_low(T, c):
                pool.wait_ge(at_hi_done, T * C + c + 1)
                pool.tensor_tensor(at_lo[:, c, :], att[:, c, :], at_hi[:, c, :].bitcast(F32),
                                   ALU.subtract).then_inc(at_lo_done, 1)

            def add_bout(T, j):
                pool.wait_ge(z2_done, T * TB + j + 1)
                pool.tensor_tensor(x1[:, j, :], x1[:, j, :], bout_row[:, :], ALU.add).then_inc(bout_added, 1)

            pool.wait_ge(setup_done, 1)

            def iteration(t, b, bf, has_f, has_a, has_b):
                if has_f:
                    for j in range(TB):
                        square(t + 1, j)
                if has_b:
                    for j in range(TB):
                        add_bout(t - 1, j)
                if has_a:
                    for c in range(C):
                        att_low(t, c)
                if has_f:
                    for j in range(TB):
                        q_low(t + 1, j)

            iterations(pool, iteration)

        PARAMS = 16 * (2 * HC + 4 + 10)
        CTX, KNORM, KREADY = [0] * NB, [0] * NB, [0] * NB

        def vector_setup(dve):
            n = [0]

            def step(ins):
                ins.then_inc(setup_dve, 1)
                n[0] += 1
                dve.wait_ge(setup_dve, n[0])

            dve.wait_ge(consts, 2 + C)
            step(dve.tensor_scalar(neg_ident[:, :], ident[:, :], -1.0, None, ALU.mult))
            step(dve.tensor_copy(bc_sel[:, :, :], bc_sel_f[:, :, :]))
            step(dve.tensor_tensor(pair_eye, ident[:, 0:M], ident[:, M:2 * M], ALU.add))
            ctx_t, ks, ks2 = hid[:, 0, :], hid[:, 1, :], hid[:, 2, :]
            heads = lambda a: a.rearrange("p (h d) -> p h d", h=H)
            per_head = lambda a: a.unsqueeze(2).broadcast_to([P, H, HD])
            on_heads = lambda a: a.unsqueeze(1).broadcast_to([P, H, HD])
            for b in range(NB):
                dve.wait_ge(setup_pe, 3 * b + 1)
                step(dve.tensor_copy(ctx_t, TR[0][:, :]))
                CTX[b] = n[0]
                dve.wait_ge(setup_pe, 3 * b + 2)
                step(dve.tensor_copy(v_kv[b][:, :], PJ[1][:, :]))
                step(dve.tensor_copy(ks, PJ[0][:, :]))
                step(dve.tensor_reduce(ssq[:, 1, :], heads(ks), AX.X, ALU.add))
                step(dve.tensor_scalar(ssq[:, 1, :], ssq[:, 1, :], 1.0 / HD, None, ALU.mult))
                step(dve.tensor_tensor(heads(ks), heads(ks), per_head(ssq[:, 1, :]), ALU.subtract))
                step(dve.tensor_tensor(ks2, ks, ks, ALU.mult))
                step(dve.tensor_reduce(ssq[:, 0, :], heads(ks2), AX.X, ALU.add))
                KNORM[b] = n[0]
                dve.wait_ge(setup_act, 2 * b + 2)
                y, a, c2 = lnq[:, 1, 0:H], lnq[:, 2, 0:H], lnq[:, 3, 0:H]
                step(dve.tensor_tensor(a, y, y, ALU.mult))
                step(dve.scalar_tensor_tensor(out=a, in0=ssq[:, 0, :], scalar=EPS * HD, in1=a,
                                              op0=ALU.add, op1=ALU.mult))
                step(dve.tensor_scalar(a, a, -0.5 / HD, 1.5, ALU.mult, ALU.add))
                step(dve.tensor_tensor(c2, y, a, ALU.mult))
                step(dve.tensor_tensor(heads(ks), heads(ks), per_head(c2), ALU.mult))
                if b == 0:
                    dve.wait_ge(params_loaded, PARAMS)
                step(dve.tensor_tensor(heads(ks), heads(ks), on_heads(gk_row[:, :]), ALU.mult))
                step(dve.tensor_tensor(heads(ks), heads(ks), on_heads(bk_row[:, :]), ALU.add))
                KREADY[b] = n[0]
                dve.wait_ge(setup_pe, 3 * b + 3)
                kt = TR[1][:, :].rearrange("p (c n) -> p c n", c=C)
                for i in range(HC):
                    rows = slice(HD * i, HD * (i + 1))
                    step(dve.tensor_copy(k_hi[b][rows, :, i, :], kt[rows]))
                    step(dve.tensor_tensor(k_lo[b][rows, :, i, :], kt[rows], k_hi[b][rows, :, i, :].bitcast(F32),
                                           ALU.subtract))
            dve.wait_ge(wq_loaded, 16)
            wqh = x1[:, :, :].rearrange("p c (h d) -> p (c h) d", h=H)
            mean = lnq[:, 0, :]
            step(dve.tensor_reduce(mean, wqh, AX.X, ALU.add))
            step(dve.tensor_scalar(mean, mean, 1.0 / HD, None, ALU.mult))
            step(dve.tensor_tensor(wqh, wqh, mean.unsqueeze(2).broadcast_to([P, C * H, HD]), ALU.subtract))
            step(dve.tensor_copy(wq_hi[:, :, :], x1[:, :, :]))
            step(dve.tensor_tensor(wq_lo[:, :, :], x1[:, :, :], wq_hi[:, :, :].bitcast(F32), ALU.subtract))
            dve.wait_ge(wo_loaded, 32)
            step(dve.tensor_copy(wo_hi[:, :, :], xin[:, :, :]))
            step(dve.tensor_tensor(wo_lo[:, :, :], xin[:, :, :], wo_hi[:, :, :].bitcast(F32), ALU.subtract))
            wst = z2[:, 0, 0:C * M].rearrange("p (c m) -> p c m", c=C)
            for half in range(2):
                step(dve.tensor_copy(win_hi[:, :, half, :], wst))
                step(dve.tensor_tensor(win_lo[:, :, half, :], wst, win_hi[:, :, half, :].bitcast(F32), ALU.subtract))
            for hh in range(HH):
                step(dve.tensor_scalar(w2_diag[:, hh, :], pair_eye, w2_col[:, hh:hh + 1], None, ALU.mult))
            dve.tensor_copy(rden[:, 0:1], ident[:, 0:1]).then_inc(setup_done, 1)

        @block.vector
        def _(dve):
            vector_setup(dve)

            def newton(buf, v, n_in, act_sem, act_value, step_sem, base):
                y, a, c2 = buf[:, 1, :], buf[:, 2, :], buf[:, 3, :]
                dve.wait_ge(act_sem, act_value)
                dve.tensor_tensor(a, y, y, ALU.mult).then_inc(step_sem, 1)
                dve.wait_ge(step_sem, base + 1)
                dve.scalar_tensor_tensor(out=a, in0=v, scalar=EPS * n_in, in1=a, op0=ALU.add,
                                         op1=ALU.mult).then_inc(step_sem, 1)
                dve.wait_ge(step_sem, base + 2)
                dve.tensor_scalar(a, a, -0.5 / n_in, 1.5, ALU.mult, ALU.add).then_inc(step_sem, 1)
                dve.wait_ge(step_sem, base + 3)
                dve.tensor_tensor(c2, y, a, ALU.mult).then_inc(step_sem, 1)
                dve.wait_ge(step_sem, base + 4)

            def aggregate(bn, mv, bn_sem, mv_sem, count):
                dve.wait_ge(bn_sem, count)
                dve.tensor_copy(spare[:, :], bn[:, 0, 0:1])
                for j in range(TB):
                    dve.bn_aggr(mv[:, j, :], bn[:, j, :]).then_inc(mv_sem, 1)

            def stats1(T):
                for j in range(TB):
                    dve.wait_ge(x_loaded[j], T * 16 + 16)
                    dve.bn_stats(bn1[:, j, :], xin[:, j, :]).then_inc(bn1_done, 1)
                aggregate(bn1, mv1, bn1_done, mv1_done, T * TB + TB)

            def norm1(T):
                newton(ln1, mv1[:, :, 1], 1, ln1_act, T * 2 + 2, ln1_step, T * 4)
                for j in range(TB):
                    dve.tensor_scalar(xin[:, j, :], xin[:, j, :], mv1[:, j, 0:1], ln1[:, 3, j:j + 1],
                                      ALU.subtract, ALU.mult).then_inc(z1_done, 1)

            def z1_low(T, j):
                dve.wait_ge(zt_hi_done, T * TB + j + 1)
                dve.tensor_tensor(zt_lo[:, j % 2, :, :].rearrange("p c n -> p (c n)"), TR[j % 2][:, :],
                                  zt_hi[:, j % 2, :, :].rearrange("p c n -> p (c n)").bitcast(F32),
                                  ALU.subtract).then_inc(zt_lo_done, 1)

            def sum_squares(T, j):
                dve.wait_ge(sq_done, T * TB + j + 1)
                dve.tensor_reduce(ssq[:, j, :], sq[:, :].rearrange("p (h d) -> p h d", h=H), AX.X,
                                  ALU.add).then_inc(ssq_done, 1)

            def normq(T):
                newton(lnq, ssq[:, :, :].rearrange("p j h -> p (j h)"), HD, lnq_act, T * 2 + 2, lnq_step, T * 4)
                for j in range(TB):
                    uj = u[:, j, :].rearrange("p (h d) -> p h d", h=H)
                    dve.tensor_tensor(uj, uj, lnq[:, 3, j * H:(j + 1) * H].unsqueeze(2).broadcast_to([P, H, HD]),
                                      ALU.mult).then_inc(un_done, 1)

            def q_full(T, j):
                dve.wait_ge(qt_hi_done, T * TB + j + 1)
                dve.tensor_scalar(u[:, j, :], TR[j % 2][:, :], gq_col[:, 0:1], bq_col[:, 0:1], ALU.mult,
                                  ALU.add).then_inc(qf_done, 1)

            def row_max(T, n):
                j, c = n // C, n % C
                dve.wait_ge(maxs_done, T * (TB * C) + n + 1)
                dve.tensor_reduce(mx[:, j, c * HC:(c + 1) * HC],
                                  PJ[n % 2][:, :].rearrange("p (i n) -> p i n", i=HC), AX.X,
                                  ALU.max).then_inc(mx_done, 1)

            def move_mxt(T):
                dve.wait_ge(mx_turned, T + 1)
                dve.tensor_copy(mxt[:, :], TR[0][:, :]).then_inc(mxt_done, 1)

            def reciprocal(t):
                dve.wait_ge(pv_done, t * H + H)
                dve.reciprocal(rden[:, :], DEN[:, :]).then_inc(rden_done, 1)
                dve.wait_ge(rden_done, t + 1)
                dve.tensor_copy(rden_hi[:, :], rden[:, :]).then_inc(rden_hi_done, 1)
                dve.wait_ge(rden_hi_done, t + 1)
                dve.tensor_tensor(rden_lo[:, :], rden[:, :], rden_hi[:, :].bitcast(F32),
                                  ALU.subtract).then_inc(rden_lo_done, 1)

            def normalise(t, c):
                dve.wait_ge(spread_done, t * C + c + 1)
                dve.wait_ge(att_moved, t * C + c + 1)
                dve.tensor_tensor(att[:, c, :], PJ[c % 2][:, :], att[:, c, :], ALU.mult).then_inc(att_done, 1)

            def residual1(T, j):
                dve.wait_ge(o_done, T * TB + j + 1)
                dve.wait_ge(xr_loaded[j], T * 16 + 16)
                dve.tensor_tensor(x1[:, j, :], PJ[j % 2][:, :], x1[:, j, :], ALU.add).then_inc(x1_done, 1)
                dve.wait_ge(x1_done, T * TB + j + 1)
                dve.bn_stats(bn2[:, j, :], x1[:, j, :]).then_inc(bn2_done, 1)
                if j == TB - 1:
                    aggregate(bn2, mv2, bn2_done, mv2_done, T * TB + TB)

            def norm2(T):
                newton(ln2, mv2[:, :, 1], 1, ln2_act, T * 2 + 2, ln2_step, T * 4)

            def z2_norm(T, j):
                if j >= 2:
                    dve.wait_ge(z2_turned, T * TB + j - 1)
                dve.tensor_scalar(z2[:, j % 2, :], x1[:, j, :], mv2[:, j, 0:1], ln2[:, 3, j:j + 1],
                                  ALU.subtract, ALU.mult).then_inc(z2_done, 1)

            def z2_low(T, j):
                cols = slice(j * P, (j + 1) * P)
                dve.wait_ge(z2t_hi_done, T * TB + j + 1)
                dve.tensor_tensor(z2t_lo[:, :, cols], TR[j % 2][:, :].rearrange("p (c n) -> p c n", c=C),
                                  z2t_hi[:, :, cols].bitcast(F32), ALU.subtract).then_inc(z2t_lo_done, 1)

            def residual2(T, j):
                dve.wait_ge(y_done, T * TB + j + 1)
                dve.wait_ge(bout_added, T * TB + j + 1)
                dve.tensor_tensor(x1[:, j, :], PJ[j % 2][:, :], x1[:, j, :], ALU.add).then_inc(out_done, 1)

            def iteration(t, b, bf, has_f, has_a, has_b):
                F, B = t + 1, t - 1
                for k in range(H):
                    if has_f and k == 0:
                        stats1(F)
                    if has_b and k < TB:
                        residual1(B, k)
                    if has_f and k == 2:
                        norm1(F)
                    if has_f and k in (4, 6):
                        z1_low(F, k - 4)
                        z1_low(F, k - 4 + 1)
                    if has_b and k == 6:
                        norm2(B)
                        z2_norm(B, 0)
                        z2_norm(B, 1)
                    if has_f and 5 <= k <= 8:
                        sum_squares(F, k - 5)
                    if has_b and k == 8:
                        z2_low(B, 0)
                        z2_low(B, 1)
                        z2_norm(B, 2)
                        z2_norm(B, 3)
                    if has_b and k == 9:
                        z2_low(B, 2)
                        z2_low(B, 3)
                    if has_f and k == 10:
                        normq(F)
                if has_a:
                    reciprocal(t)
                if has_b:
                    for j in range(TB):
                        residual2(B, j)
                if has_a:
                    for c in range(C):
                        normalise(t, c)
                if has_f:
                    for j in range(TB):
                        q_full(F, j)
                    for n in range(TB * C):
                        row_max(F, n)
                    move_mxt(F)

            iterations(dve, iteration)

        @block.scalar
        def _(act):
            def rsqrt_guess(v, out2, n_in, in_sem, in_value, act_sem, act_value):
                act.wait_ge(in_sem, in_value)
                act.activation(out2[0], v, ACT.Ln, bias=EPS, scale=1.0 / n_in).then_inc(act_sem, 1)
                act.wait_ge(act_sem, act_value - 1)
                act.activation(out2[1], out2[0], ACT.Exp, scale=-0.5).then_inc(act_sem, 1)

            act.preload_act_table_set("natural_log_exp_and_others")
            for b in range(NB):
                rsqrt_guess(ssq[:, 0, :], (lnq[:, 0, 0:H], lnq[:, 1, 0:H]), HD, setup_dve, KNORM[b],
                            setup_act, 2 * b + 2)
            act.wait_ge(setup_done, 1)

            def norm1(T):
                rsqrt_guess(mv1[:, :, 1], (ln1[:, 0, :], ln1[:, 1, :]), 1, mv1_done, T * TB + TB, ln1_act, T * 2 + 2)

            def norm2(T):
                rsqrt_guess(mv2[:, :, 1], (ln2[:, 0, :], ln2[:, 1, :]), 1, mv2_done, T * TB + TB, ln2_act, T * 2 + 2)

            def normq(T):
                rsqrt_guess(ssq[:, :, :].rearrange("p j h -> p (j h)"), (lnq[:, 0, :], lnq[:, 1, :]), HD,
                            ssq_done, T * TB + TB, lnq_act, T * 2 + 2)

            def z1_high(T, j):
                act.wait_ge(z1_turned, T * TB + j + 1)
                if j >= 2:
                    act.wait_ge(q_done, T * TB + j - 1)
                act.activation(zt_hi[:, j % 2, :, :].rearrange("p c n -> p (c n)"), TR[j % 2][:, :],
                               ACT.Copy).then_inc(zt_hi_done, 1)

            def move_u(T, j):
                act.wait_ge(q_done, T * TB + j + 1)
                if not first(T):
                    act.wait_ge(qt_lo_done, T * TB + j + 1 - TB)
                act.activation(u[:, j, :], PJ[j % 2][:, :], ACT.Copy).then_inc(u_done, 1)

            def q_high(T, j):
                act.wait_ge(q_turned, T * TB + j + 1)
                act.activation(qt_hi[:, :, j * P:(j + 1) * P], TR[j % 2][:, :].rearrange("p (c n) -> p c n", c=C),
                               ACT.Identity, bias=bq_col[:, 0:1], scale=gq_col[:, 0:1]).then_inc(qt_hi_done, 1)

            def exponential(t, h):
                act.wait_ge(scores_done, t * H + h + 1)
                if h >= PR:
                    act.wait_ge(pv_done, t * H + h + 1 - PR)
                act.activation(prob[:, h % PR, :], S[h % 2][:, :], ACT.Exp, scale=SCALE).then_inc(exp_done, 1)

            def move_att(t, c):
                act.wait_ge(pv_done, t * H + (c + 1) * HC)
                if not first(t):
                    act.wait_ge(at_lo_done, t * C + c + 1 - C)
                act.activation(att[:, c, :], AT[:, :], ACT.Copy).then_inc(att_moved, 1)

            def att_high(t, c):
                act.wait_ge(att_done, t * C + c + 1)
                act.activation(at_hi[:, c, :], att[:, c, :], ACT.Copy).then_inc(at_hi_done, 1)

            def z2_high(T, j):
                act.wait_ge(z2_turned, T * TB + j + 1)
                act.activation(z2t_hi[:, :, j * P:(j + 1) * P], TR[j % 2][:, :].rearrange("p (c n) -> p c n", c=C),
                               ACT.Copy).then_inc(z2t_hi_done, 1)

            def move_s(T):
                act.wait_ge(s_mm_done, T + 1)
                act.activation(s_in[:, :], TR[0][:, :], ACT.Identity, bias=bin_col[:, 0:1]).then_inc(s_done, 1)

            def hidden(T, hh):
                act.wait_ge(s_done, T + 1)
                if hh >= RR:
                    act.wait_ge(hsum_done, T * HH + hh + 1 - RR)
                act.activation(hid[:, hh % RR, :], s_in[:, :], ACT.Relu, bias=b1_col[:, hh:hh + 1],
                               scale=w1_col[:, hh:hh + 1]).then_inc(hid_done, 1)

            def move_g(T):
                act.wait_ge(hsum_done, T * HH + HH)
                act.activation(g[:, :], TR[1][:, :], ACT.Identity, bias=b2_col[:, 0:1]).then_inc(g_done, 1)

            def iteration(t, b, bf, has_f, has_a, has_b):
                F, B = t + 1, t - 1
                for k in range(H):
                    if has_a:
                        exponential(t, k)
                    if has_a and k in (5, 9, 13):
                        move_att(t, (k - 5) // 4)
                    if has_f and k == 1:
                        norm1(F)
                    if has_f and k in (4, 6):
                        z1_high(F, (k - 4))
                        z1_high(F, (k - 4) + 1)
                    if has_b and k == 6:
                        norm2(B)
                    if has_f and 5 <= k <= 8:
                        move_u(F, k - 5)
                    if has_b and k in (8, 9):
                        z2_high(B, 2 * (k - 8))
                        z2_high(B, 2 * (k - 8) + 1)
                    if has_b and k == 10:
                        move_s(B)
                    if has_f and k == 10:
                        normq(F)
                    if has_b and 10 <= k <= 13:
                        hidden(B, 2 * (k - 10))
                        hidden(B, 2 * (k - 10) + 1)
                    if has_b and k == 14:
                        move_g(B)
                if has_a:
                    move_att(t, C - 1)
                    for c in range(C):
                        att_high(t, c)
                if has_f:
                    for j in range(TB):
                        q_high(F, j)

            iterations(act, iteration)

        @block.tensor
        def _(pe):
            def three_pass(dst, pairs, start=True, stop=True):
                terms = [t for (lh, ll, rh, rl) in pairs for t in ((lh, rh), (lh, rl), (ll, rh))]
                for n, (l, r) in enumerate(terms):
                    ins = pe.matmul(dst, l, r, start=start and n == 0, stop=stop and n == len(terms) - 1)
                return ins

            wk, wv, ctx_in = att, u, prob
            ctx_t = hid[:, 0, :].rearrange("p (c n) -> p c n", c=C)
            pe.wait_ge(consts, 2 + C)
            pe.wait_ge(kvin_loaded, 48)
            for b in range(NB):
                if b:
                    pe.wait_ge(setup_dve, KREADY[b - 1])
                for c in range(C):
                    ins = pe.transpose(TR[0][:, c * P:(c + 1) * P], ctx_in[:, b, c * P:(c + 1) * P], ident[:, :])
                ins.then_inc(setup_pe, 1)
                pe.wait_ge(setup_dve, CTX[b])
                for dst, w in ((PJ[0], wk), (PJ[1], wv)):
                    for c in range(C):
                        ins = pe.matmul(dst[:, :], ctx_t[:, c, :], w[:, c, :], start=c == 0, stop=c == C - 1)
                ins.then_inc(setup_pe, 1)
                pe.wait_ge(setup_dve, KREADY[b])
                for c in range(C):
                    ins = pe.transpose(TR[1][:, c * P:(c + 1) * P], hid[:, 1, c * P:(c + 1) * P], ident[:, :])
                ins.then_inc(setup_pe, 1)
            pe.wait_ge(setup_done, 1)
            pe.wait_ge(params_loaded, PARAMS)

            def turn(dst, src, done):
                for c in range(C):
                    ins = pe.transpose(dst[:, c * P:(c + 1) * P], src[:, c * P:(c + 1) * P], ident[:, :])
                ins.then_inc(done, 1)

            def turn_z1(T, j):
                pe.wait_ge(z1_done, T * TB + j + 1)
                turn(TR[j % 2], xin[:, j, :], z1_turned)

            def project_q(T, j):
                pe.wait_ge(zt_lo_done, T * TB + j + 1)
                three_pass(PJ[j % 2][:, :], [(zt_hi[:, j % 2, c, :], zt_lo[:, j % 2, c, :], wq_hi[:, c, :], wq_lo[:, c, :])
                                             for c in range(C)]).then_inc(q_done, 1)

            def turn_q(T, j):
                pe.wait_ge(un_done, T * TB + j + 1)
                turn(TR[j % 2], u[:, j, :], q_turned)

            def max_scores(T, n, b):
                j, c = n // C, n % C
                pe.matmul(PJ[n % 2][:, :], qt_hi[:, c, j * P:(j + 1) * P],
                          k_hi[b][:, c, :, :].rearrange("p i n -> p (i n)"), start=True, stop=True).then_inc(maxs_done, 1)

            def turn_max(T):
                pe.wait_ge(mx_done, T * (TB * C) + TB * C)
                for j in range(TB):
                    ins = pe.transpose(TR[0][:, j * P:(j + 1) * P], mx[:, j, :], ident[:, :])
                ins.then_inc(mx_turned, 1)

            def scores(t, b, h):
                c, i = h // HC, h % HC
                if h == 0:
                    pe.wait_ge(qt_lo_done, t * TB + TB)
                    pe.wait_ge(mxt_done, t + 1)
                if not (first(t) and h < 2):
                    pe.wait_ge(exp_done, t * H + h - 1)
                dst = S[h % 2]
                pe.matmul(dst[:, :], neg_ident[:, h:h + 1].broadcast_to([P, P]), mxt[:, :], start=True, stop=False)
                three_pass(dst[:, :], [(k_hi[b][:, c, i, :], k_lo[b][:, c, i, :], qt_hi[:, c, :], qt_lo[:, c, :])],
                           start=False).then_inc(scores_done, 1)

            def values(t, b, h):
                c, i = h // HC, h % HC
                pe.wait_ge(exp_done, t * H + h + 1)
                if i == 0 and not (first(t) and c == 0):
                    pe.wait_ge(att_moved, t * C + c)
                if h == 0 and not first(t):
                    pe.wait_ge(rden_done, t)
                rows = slice(HD * i, HD * (i + 1))
                pe.matmul(AT[rows, :], v_kv[b][:, h * HD:(h + 1) * HD], prob[:, h % PR, :], start=True, stop=True)
                pe.matmul(DEN[rows, :], den_sel[:, c, :], prob[:, h % PR, :], start=c == 0,
                          stop=c == C - 1).then_inc(pv_done, 1)

            def spread(t, c):
                if c == 0:
                    pe.wait_ge(rden_lo_done, t + 1)
                pe.matmul(PJ[c % 2][:, :], bc_sel[:, c, :], rden_hi[:, :], start=True, stop=False)
                pe.matmul(PJ[c % 2][:, :], bc_sel[:, c, :], rden_lo[:, :], start=False, stop=True).then_inc(spread_done, 1)

            def project_o(T, j):
                cols = slice(j * P, (j + 1) * P)
                if j == 0:
                    pe.wait_ge(at_lo_done, T * C + C)
                three_pass(PJ[j % 2][:, :], [(at_hi[:, c, cols], at_lo[:, c, cols], wo_hi[:, c, :], wo_lo[:, c, :])
                                             for c in range(C)]).then_inc(o_done, 1)

            def turn_z2(T, j):
                pe.wait_ge(z2_done, T * TB + j + 1)
                turn(TR[j % 2], z2[:, j % 2, :], z2_turned)

            def project_s(T):
                pe.wait_ge(z2t_lo_done, T * TB + TB)
                both = lambda w, c: w[:, c, :, :].rearrange("p a m -> p (a m)")
                three_pass(TR[0][:, :], [(both(win_hi, c), both(win_lo, c), z2t_hi[:, c, :], z2t_lo[:, c, :])
                                         for c in range(C)]).then_inc(s_mm_done, 1)

            def sum_hidden(T, hh):
                half = hh % 2
                pe.wait_ge(hid_done, T * HH + hh + 1)
                pe.matmul(TR[1][M * half:M * (half + 1), :], w2_diag[:, hh, :], hid[:, hh % RR, :],
                          start=hh < 2, stop=hh >= HH - 2).then_inc(hsum_done, 1)

            def project_y(T, j):
                if j == 0:
                    pe.wait_ge(g_done, T + 1)
                pe.matmul(PJ[j % 2][:, :], g[:, j * P:(j + 1) * P], wout2[:, :], start=True, stop=True).then_inc(y_done, 1)

            def iteration(t, b, bf, has_f, has_a, has_b):
                F, B = t + 1, t - 1
                for k in range(H):
                    if has_a:
                        scores(t, b, k)
                        if k >= 2:
                            values(t, b, k - 2)
                    if has_b and k < TB:
                        if k >= 2:
                            pe.wait_ge(x1_done, B * TB + k - 1)
                        elif has_a:
                            pe.wait_ge(mx_done, t * (TB * C) + TB * C)
                        else:
                            pe.wait_ge(att_done, B * C + C)
                        project_o(B, k)
                    if has_f and k in (4, 6):
                        for j in (k - 4, k - 3):
                            if k == 6:
                                pe.wait_ge(zt_lo_done, F * TB + j - 1)
                            elif not first(F):
                                pe.wait_ge(qf_done, t * TB + TB)
                                pe.wait_ge(mxt_done, t + 1)
                            turn_z1(F, j)
                    if has_f and 5 <= k <= 8:
                        j = k - 5
                        if j >= 2:
                            pe.wait_ge(u_done, F * TB + j - 1)
                        elif has_b:
                            pe.wait_ge(x1_done, B * TB + TB)
                        elif has_a:
                            pe.wait_ge(mx_done, t * (TB * C) + TB * C)
                        project_q(F, j)
                    if has_b and k in (8, 9):
                        for j in (2 * (k - 8), 2 * (k - 8) + 1):
                            if j >= 2:
                                pe.wait_ge(z2t_lo_done, B * TB + j - 1)
                            elif has_f:
                                pe.wait_ge(zt_lo_done, F * TB + TB)
                            elif has_a:
                                pe.wait_ge(qf_done, t * TB + TB)
                                pe.wait_ge(mxt_done, t + 1)
                            else:
                                pe.wait_ge(g_done, B)
                            turn_z2(B, j)
                    if has_b and k == 10:
                        project_s(B)
                    if has_b and 11 <= k <= 14:
                        sum_hidden(B, 2 * (k - 11))
                        sum_hidden(B, 2 * (k - 11) + 1)
                if has_a:
                    values(t, b, H - 2)
                    values(t, b, H - 1)
                if has_b:
                    for j in range(TB):
                        if j >= 2:
                            pe.wait_ge(out_done, B * TB + j - 1)
                        elif has_f:
                            pe.wait_ge(u_done, F * TB + TB)
                        else:
                            pe.wait_ge(x1_done, B * TB + TB)
                        project_y(B, j)
                if has_a:
                    for c in range(C):
                        if c >= 2:
                            pe.wait_ge(att_done, t * C + c - 1)
                        elif has_b:
                            pe.wait_ge(out_done, B * TB + TB)
                        else:
                            pe.wait_ge(u_done, F * TB + TB)
                        spread(t, c)
                if has_f:
                    for j in range(TB):
                        if j >= 2:
                            pe.wait_ge(qf_done, F * TB + j - 1)
                        elif has_b:
                            pe.wait_ge(g_done, B + 1)
                        else:
                            pe.wait_ge(zt_lo_done, F * TB + TB)
                        turn_q(F, j)
                    for n in range(TB * C):
                        if n % C == 0:
                            pe.wait_ge(qt_hi_done, F * TB + n // C + 1)
                        if n >= 2:
                            pe.wait_ge(mx_done, F * (TB * C) + n - 1)
                        elif has_a:
                            pe.wait_ge(att_done, t * C + C)
                        max_scores(F, n, bf)
                    pe.wait_ge(qf_done, F * TB + TB)
                    turn_max(F)

            iterations(pe, iteration)


_INS = ['x', 'ctx_1024', 'L0_xattn_Wq', 'L0_xattn_Wk', 'L0_xattn_Wv', 'L0_xattn_Wo', 'L0_xattn_gq', 'L0_xattn_bq',
        'L0_xattn_gk', 'L0_xattn_bk', 'L0_ffn_Win', 'L0_ffn_bin_', 'L0_ffn_W1', 'L0_ffn_b1', 'L0_ffn_W2',
        'L0_ffn_b2', 'L0_ffn_Wout', 'L0_ffn_bout']


def kernel(**inputs):
    import numpy as _np
    import concourse.bacc as _bacc
    from concourse import mybir as _mybir
    from concourse.bass_utils import run_bass_kernel_spmd as _run

    nc = _bacc.Bacc("TRN2", target_bir_lowering=False, num_devices=1)
    arrays, args = {}, []
    for name in _INS:
        a = _np.ascontiguousarray(inputs[name])
        arrays[f"in_{name}_dram"] = a
        args.append(nc.dram_tensor(f"in_{name}_dram", a.shape, _mybir.dt.from_np(a.dtype), kind="ExternalInput").ap())
    args.append(nc.dram_tensor("out_0_dram", inputs['x'].shape, _mybir.dt.float32, kind="ExternalOutput").ap())
    build_program(nc, *args)
    r = _run(nc, [arrays], core_ids=[0])
    return r.results[0]["out_0_dram"]
```

```python
import concourse.bass as bass
from concourse import mybir
from contextlib import ExitStack

F32 = mybir.dt.float32
F32R = mybir.dt.float32r
ALU = mybir.AluOpType
ACT = mybir.ActivationFunctionType
AX = mybir.AxisListType

P = 128
D = 512
C = D // P
H = 16
HD = D // H
HC = H // C
NB = 2
SQ = 2048
KV = 128
TB = 4
TOK = TB * P
BLOCKS = NB * SQ // TOK
M = 64
INNER = 16
HH = INNER // 2
EPS = 1e-5
SCALE = HD ** -0.5
PR = 4
RR = 4
G = H // HC
PAIRS = H // 2
MAX_TILES = G // 2 * TB
NEYES = 4
NCONSTS = 3 + C + NB


def build_program(nc, x, ctx_kv, Wq, Wk, Wv, Wo, gq, bq, gk, bk, Win, bin_, W1, b1, W2, b2, Wout, bout, out):
    with ExitStack() as stack:
        def sb(name, shape, dt=F32):
            return stack.enter_context(nc.sbuf_tensor(name, shape, dt))

        def bank(name):
            return stack.enter_context(nc.psum_tensor(name, [P, D], F32))

        def sem(name):
            return stack.enter_context(nc.semaphore(name))

        wq_hi = sb("wq_hi", [P, C, D], F32R)
        wq_lo = sb("wq_lo", [P, C, D], F32R)
        wo_hi = sb("wo_hi", [P, C, D], F32R)
        wo_lo = sb("wo_lo", [P, C, D], F32R)
        win_hi = sb("win_hi", [P, C, 2, M], F32R)
        win_lo = sb("win_lo", [P, C, 2, M], F32R)
        wout2 = sb("wout2", [P, D])
        w2_diag = sb("w2_diag", [P, HH, M])
        bout_row = sb("bout_row", [P, D])
        k_stack = [sb(f"k_stack{b}", [P, H, KV], F32R) for b in range(NB)]
        v_kv = [sb(f"v_kv{b}", [P, D]) for b in range(NB)]
        gq_col = sb("gq_col", [P, 1])
        bq_col = sb("bq_col", [P, 1])
        gk_row = sb("gk_row", [P, HD])
        bk_row = sb("bk_row", [P, HD])
        bin_col = sb("bin_col", [P, 1])
        w1_col = sb("w1_col", [P, HH])
        b1_col = sb("b1_col", [P, HH])
        w2_col = sb("w2_col", [P, HH])
        b2_col = sb("b2_col", [P, 1])
        ident = sb("ident", [P, P])
        den_sel = sb("den_sel", [P, C, HD])
        bc_sel = sb("bc_sel", [P, C, P], F32R)
        xin = sb("xin", [P, TB, D])
        zt_hi = sb("zt_hi", [P, 2, C, P], F32R)
        zt_lo = sb("zt_lo", [P, 2, C, P], F32R)
        u = sb("u", [P, TB, D])
        sq = sb("sq", [P, D])
        qt_hi = sb("qt_hi", [P, HC, TOK], F32R)
        qt_lo = sb("qt_lo", [P, HC, TOK], F32R)
        q_stack = sb("q_stack", [P, H, TOK], F32R)
        mx = sb("mx", [P, TB, H])
        mxt = sb("mxt", [H // 2, 2, TOK], F32R)
        prob = sb("prob", [P, PR, TOK])
        att = sb("att", [P, C, TOK])
        at_hi = sb("at_hi", [P, C, TOK], F32R)
        at_lo = sb("at_lo", [P, C, TOK], F32R)
        rden = sb("rden", [P, TOK])
        bc_sel_f = rden[:, :].rearrange("p (c n) -> p c n", c=C)
        rden_hi = sb("rden_hi", [P, TOK], F32R)
        rden_lo = sb("rden_lo", [P, TOK], F32R)
        x1 = sb("x1", [P, TB, D])
        z2 = sb("z2", [P, 2, D])
        z2t_hi, z2t_lo = at_hi, at_lo
        s_in = sb("s_in", [P, TOK])
        pair_eye = s_in[:, 0:M]
        hid = sb("hid", [P, RR, TOK])
        g_mid = sb("g_mid", [P, TOK])
        bn1 = sb("bn1", [P, TB, 6])
        mv1 = sb("mv1", [P, TB, 2])
        bn2 = sb("bn2", [P, TB, 6])
        mv2 = sb("mv2", [P, TB, 2])
        ssq = sb("ssq", [P, TB, H])
        ln1 = sb("ln1", [P, 4, TB])
        ln2 = sb("ln2", [P, 4, TB])
        spare = sb("spare", [P, 1])
        lnq = sb("lnq", [P, 4, TB * H])
        kst = z2[:, 0, 0:6 * NB * H].rearrange("p (k h) -> p k h", k=6)

        AT = bank("AT")
        DEN = bank("DEN")
        banks = [bank(f"bank{n}") for n in range(6)]
        z1_bank = [banks[n] for n in (4, 1, 4, 1)]
        q_bank = [banks[n] for n in (4, 5, 5, 4)]
        qt_bank = [banks[n] for n in (5, 1, 4, 3)]
        maxs_bank = [[banks[n] for n in (5, 0, 3, 5)],
                     [banks[n] for n in (3, 5, 0, 5)],
                     [banks[n] for n in (2, 5, 3, 0)],
                     [banks[n] for n in (0, 2, 5, 5)]]
        mxt_bank = [banks[n] for n in (2, 0)]
        score_bank = [banks[n] for n in (2, 3, 1, 2, 3, 5, 0, 2, 2, 1, 0, 5, 4, 1, 4, 3)]
        spread_bank = [banks[n] for n in (0, 5, 0, 3)]
        o_bank = [banks[n] for n in (1, 4, 0, 4)]
        z2_bank = [banks[n] for n in (5, 1, 0, 4)]
        s_bank, g_bank = banks[2], banks[2]
        y_bank = [banks[n] for n in (2, 5, 2, 2)]

        names = """eyes consts params_loaded kv_loaded wv_loaded wq_loaded wo_loaded ctx_turned ctx_moved kv_projected keys_moved
            values_moved wq_step wq_hi_done wq_split wo_hi_done weights_split key_step key_guess keys_turned
            keys_hi_done keys_split keys_stacked bn1_done mv1_done ln1_act ln1_step z1_done z1_turned zt_hi_done
            zt_lo_done q_done u_done sq_done ssq_done lnq_act lnq_step un_done q_turned qt_hi_done qf_done qt_lo_done
            scores_done exp_done pv_done att_moved rden_done rden_hi_done
            rden_lo_done spread_done att_done at_hi_done at_lo_done o_done x1_done bn2_done mv2_done ln2_act ln2_step
            z2_done bout_added z2_turned z2t_hi_done z2t_lo_done s_mm_done s_done hid_done hsum_done g_done y_done
            out_done""".split()
        sems = {name: sem(name) for name in names}
        (eyes, consts, params_loaded, kv_loaded, wv_loaded, wq_loaded, wo_loaded, ctx_turned, ctx_moved, kv_projected, keys_moved,
         values_moved, wq_step, wq_hi_done, wq_split, wo_hi_done, weights_split, key_step, key_guess, keys_turned,
         keys_hi_done, keys_split, keys_stacked, bn1_done, mv1_done, ln1_act, ln1_step, z1_done, z1_turned, zt_hi_done,
         zt_lo_done, q_done, u_done, sq_done, ssq_done, lnq_act, lnq_step, un_done, q_turned, qt_hi_done, qf_done,
         qt_lo_done, scores_done, exp_done, pv_done, att_moved, rden_done,
         rden_hi_done, rden_lo_done, spread_done, att_done, at_hi_done, at_lo_done, o_done, x1_done, bn2_done, mv2_done,
         ln2_act, ln2_step, z2_done, bout_added, z2_turned, z2t_hi_done, z2t_lo_done, s_mm_done, s_done, hid_done,
         hsum_done, g_done, y_done, out_done) = (sems[name] for name in names)
        x_loaded = [sem(f"x_loaded{j}") for j in range(TB)]
        xr_loaded = [sem(f"xr_loaded{j}") for j in range(TB)]
        stored = [sem(f"stored{j}") for j in range(TB)]
        stacked = [sem(f"stacked{g}") for g in range(G)]
        maxs_done, mx_done, mx_turned, mxt_done, max_stacked = (
            [sem(f"{name}{half}") for half in range(2)]
            for name in ("maxs_done", "mx_done", "mx_turned", "mxt_done", "max_stacked"))

        PARAMS = 16 * (2 * HC + 4 + 10)
        WEIGHTS = 1 + 2 + HH

        block = stack.enter_context(nc.Block())

        x_t = x.rearrange("b (n j p) d -> (b n) j p d", p=P, j=TB)
        out_t = out.rearrange("b (n j p) d -> (b n) j p d", p=P, j=TB)

        wk_in, wv_in, wq_in, wo_in = att, hid, x1, x1
        ctx_in, keys = prob[:, 0:NB, :], prob[:, NB:2 * NB, :]
        ctx_t, keys2 = u[:, 0:NB, :], att[:, 0:NB, :]
        win_in = g_mid[:, 0:C * M].rearrange("p (c m) -> p c m", c=C)
        kn_hi, kn_lo = at_hi[:, 0:NB, :], at_lo[:, 0:NB, :]

        def iterations(engine, iteration, enter=lambda: None):
            per = BLOCKS // NB
            iteration(-1, 0, 0, g=True, f=True, a=False, b=False)
            iteration(0, 0, 0, g=True, f=True, a=True, b=False)
            enter()
            with engine.Fori(1, per - 1) as t:
                iteration(t, 0, 0, g=True, f=True, a=True, b=True)
            iteration(per - 1, 0, 1, g=True, f=True, a=True, b=True)
            with engine.Fori(per, BLOCKS - 2) as t:
                iteration(t, 1, 1, g=True, f=True, a=True, b=True)
            iteration(BLOCKS - 2, 1, 1, g=False, f=True, a=True, b=True)
            iteration(BLOCKS - 1, 1, 1, g=False, f=False, a=True, b=True)
            iteration(BLOCKS, 1, 1, g=False, f=False, a=False, b=True)

        def by_place(a):
            return a.rearrange("p (g i d) -> p i g d", g=G, i=HC)

        def first(t):
            return isinstance(t, int) and t <= 0

        @block.sync
        def _(sp):
            sp.dma_start(ctx_in, ctx_kv.rearrange("b k d -> k b d")).then_inc(kv_loaded, 16)
            sp.dma_start(wk_in[:, :, :], Wk.rearrange("(c p) n -> p c n", p=P)).then_inc(kv_loaded, 16)
            sp.dma_start(wq_in[:, :, :], Wq.rearrange("(c p) n -> p c n", p=P)).then_inc(wq_loaded, 16)
            for j in range(TB):
                sp.dma_start(xin[:, j, :], x_t[0, j]).then_inc(x_loaded[j], 16)
            sp.dma_start(wv_in[:, :, :], Wv.rearrange("(c p) n -> p c n", p=P)).then_inc(wv_loaded, 16)
            column = lambda a: a.rearrange("(p o) -> p o", o=1)
            row = lambda a, n: a.rearrange("(o n) -> o n", o=1).broadcast_to([P, n])
            for i in range(HC):
                rows = slice(HD * i, HD * (i + 1))
                sp.dma_start(gq_col[rows, :], column(gq)).then_inc(params_loaded, 16)
                sp.dma_start(bq_col[rows, :], column(bq)).then_inc(params_loaded, 16)
            sp.dma_start(gk_row[:, :], row(gk, HD)).then_inc(params_loaded, 16)
            sp.dma_start(bk_row[:, :], row(bk, HD)).then_inc(params_loaded, 16)
            sp.dma_start(bout_row[:, :], row(bout, D)).then_inc(params_loaded, 16)
            sp.wait_ge(eyes, NEYES)
            sp.dma_start(b2_col[0:M, :], column(b2)).then_inc(params_loaded, 16)
            for half in range(2):
                rows, units = slice(M * half, M * (half + 1)), slice(HH * half, HH * (half + 1))
                sp.dma_start(bin_col[rows, :], column(bin_)).then_inc(params_loaded, 16)
                sp.dma_start(w1_col[rows, :], W1[:, units]).then_inc(params_loaded, 16)
                sp.dma_start(b1_col[rows, :], b1[:, units]).then_inc(params_loaded, 16)
                sp.dma_start(w2_col[rows, :], W2[:, units]).then_inc(params_loaded, 16)
                sp.dma_start(wout2[rows, :], Wout).then_inc(params_loaded, 16)
            sp.wait_ge(wq_split, 2 + C)
            sp.dma_start(wo_in[:, :, :], Wo.rearrange("(c p) n -> p c n", p=P)).then_inc(wo_loaded, 16)
            sp.dma_start(win_in, Win.rearrange("(c p) m -> p c m", p=P)).then_inc(wo_loaded, 16)

            def stack_keys():
                sp.wait_ge(keys_split, NB)
                for b in range(NB):
                    for gr in range(G):
                        rows, heads = slice(HD * gr, HD * (gr + 1)), slice(HC * gr, HC * (gr + 1))
                        for part, src in enumerate((kn_hi, kn_hi, kn_lo)):
                            sp.dma_start(k_stack[b][HD * part:HD * (part + 1), heads, :].bitcast(F32),
                                         src[rows, b, :].rearrange("p (i n) -> p i n", i=HC).bitcast(F32)
                                         ).then_inc(keys_stacked, 16)

            def load_x(T, j):
                sp.wait_ge(z1_turned, T * TB + j + 1 - TB)
                sp.dma_start(xin[:, j, :], x_t[T, j]).then_inc(x_loaded[j], 16)

            def load_residual(T, j):
                if first(T):
                    if j == 0:
                        sp.wait_ge(weights_split, WEIGHTS)
                else:
                    sp.wait_ge(stored[j], T * 16)
                sp.dma_start(x1[:, j, :], x_t[T, j]).then_inc(xr_loaded[j], 16)

            def stack_q(T, gr):
                if gr == 0:
                    sp.wait_ge(qt_lo_done, T * TB + TB)
                if not first(T):
                    sp.wait_ge(scores_done, T * H + (gr + 1) * HC - H)
                rows, heads = slice(HD * gr, HD * (gr + 1)), slice(HC * gr, HC * (gr + 1))
                for part, src in enumerate((qt_hi, qt_lo, qt_hi)):
                    sp.dma_start(q_stack[HD * part:HD * (part + 1), heads, :].bitcast(F32),
                                 src[rows, :, :].bitcast(F32)).then_inc(stacked[gr], 16)

            def stack_max(T, half):
                sp.wait_ge(mxt_done[half], T + 1)
                sp.dma_start(q_stack[3 * HD:3 * HD + 1, H // 2 * half:H // 2 * (half + 1), :].bitcast(F32),
                             mxt[:, half, :].bitcast(F32)).then_inc(max_stacked[half], 16)

            def store(T, j):
                sp.wait_ge(out_done, T * TB + j + 1)
                sp.dma_start(out_t[T, j], x1[:, j, :]).then_inc(stored[j], 16)

            def iteration(t, kb, kf, g, f, a, b):
                N, F, B, prologue = t + 2, t + 1, t - 1, isinstance(t, int) and t == -1
                if g:
                    load_x(N, 0)
                    load_x(N, 1)
                    load_x(N, 2)
                if b:
                    load_residual(B, 0)
                    load_residual(B, 1)
                    load_residual(B, 2)
                if g:
                    load_x(N, 3)
                if prologue:
                    stack_keys()
                if b:
                    load_residual(B, 3)
                if a:
                    stack_max(t, 1)
                if f:
                    stack_q(F, 0)
                    stack_q(F, 1)
                if b:
                    store(B, 0)
                if f:
                    stack_q(F, 2)
                    stack_max(F, 0)
                    stack_q(F, 3)
                if b:
                    store(B, 1)
                    store(B, 2)
                    store(B, 3)

            iteration(-1, 0, 0, True, True, False, False)
            iteration(0, 0, 0, True, True, True, False)
            iteration(1, 0, 0, True, True, True, True)
            with sp.Fori(2, BLOCKS - 2) as t:
                iteration(t, 0, 0, True, True, True, True)
            iteration(BLOCKS - 2, 1, 1, False, True, True, True)
            iteration(BLOCKS - 1, 1, 1, False, False, True, True)
            iteration(BLOCKS, 1, 1, False, False, False, True)
            for j in range(TB):
                sp.wait_ge(stored[j], BLOCKS * 16)

        @block.gpsimd
        def _(pool):
            pool.memset(ident[:, :], 0.0).then_inc(eyes, 1)
            pool.memset(b2_col[:, :], 0.0).then_inc(eyes, 1)
            pool.memset(bc_sel_f[:, :, :], 0.0).then_inc(eyes, 1)
            pool.memset(den_sel[:, :, :], 0.0).then_inc(eyes, 1)
            pool.wait_ge(eyes, NEYES)
            pool.affine_select(out=ident[:, :], in_=ident[:, :], compare_op=ALU.not_equal, fill=1.0,
                               base=0, pattern=[[-1, P]], channel_multiplier=1).then_inc(consts, 1)
            sel = bc_sel_f[:, :, :].rearrange("p c (a i d) -> p c a i d", a=2, i=2)
            for a in range(2):
                pool.affine_select(out=sel[:, :, a], in_=sel[:, :, a], compare_op=ALU.not_equal, fill=1.0,
                                   base=-2 * HD * (1 - a), pattern=[[-8, C], [-HD, 2], [0, HD]],
                                   channel_multiplier=1).then_inc(consts, 1)
            for c in range(C):
                pool.memset(den_sel[:, c, 8 * c:8 * c + 8], 1.0).then_inc(consts, 1)
            for b in range(NB):
                pool.wait_ge(consts, 3 + C + b)
                pool.memset(k_stack[b][3 * HD:3 * HD + 1, :, :].bitcast(F32), -1.0).then_inc(consts, 1)

            def split_weights():
                pool.wait_ge(wo_hi_done, 3)
                pool.tensor_tensor(wo_lo[:, :, :], wo_in[:, :, :], wo_hi[:, :, :].bitcast(F32),
                                   ALU.subtract).then_inc(weights_split, 1)
                for half in range(2):
                    pool.tensor_tensor(win_lo[:, :, half, :], win_in, win_hi[:, :, half, :].bitcast(F32),
                                       ALU.subtract).then_inc(weights_split, 1)
                pool.wait_ge(params_loaded, PARAMS)
                for hh in range(HH):
                    pool.tensor_scalar(w2_diag[:, hh, :], pair_eye, w2_col[:, hh:hh + 1], 0.0, ALU.mult,
                                       ALU.add).then_inc(weights_split, 1)

            def square(T, j):
                pool.wait_ge(u_done, T * TB + j + 1)
                if not (first(T) and j == 0):
                    pool.wait_ge(ssq_done, T * TB + j)
                pool.tensor_tensor(sq[:, :], u[:, j, :], u[:, j, :], ALU.mult).then_inc(sq_done, 1)

            def q_low(T, j):
                cols = slice(j * P, (j + 1) * P)
                pool.wait_ge(qf_done, T * TB + j + 1)
                pool.tensor_tensor(qt_lo[:, :, cols], u[:, j, :].rearrange("p (i n) -> p i n", i=HC),
                                   qt_hi[:, :, cols].bitcast(F32), ALU.subtract).then_inc(qt_lo_done, 1)

            def att_low(T, c):
                pool.wait_ge(at_hi_done, T * C + c + 1)
                pool.tensor_tensor(at_lo[:, c, :], att[:, c, :], at_hi[:, c, :].bitcast(F32),
                                   ALU.subtract).then_inc(at_lo_done, 1)

            def add_bout(T, j):
                pool.wait_ge(z2_done, T * TB + j + 1)
                pool.tensor_tensor(x1[:, j, :], x1[:, j, :], bout_row[:, :], ALU.add).then_inc(bout_added, 1)

            def iteration(t, kb, kf, g, f, a, b):
                if isinstance(t, int) and t == 0:
                    split_weights()
                F, B = t + 1, t - 1
                if b:
                    att_low(B, 0)
                if f:
                    square(F, 0)
                if b:
                    att_low(B, 1)
                if f:
                    square(F, 1)
                if b:
                    att_low(B, 2)
                    att_low(B, 3)
                if f:
                    square(F, 2)
                    square(F, 3)
                if b:
                    add_bout(B, 0)
                if f:
                    q_low(F, 0)
                    q_low(F, 1)
                    q_low(F, 2)
                    q_low(F, 3)
                if b:
                    add_bout(B, 1)
                    add_bout(B, 2)
                    add_bout(B, 3)

            iterations(pool, iteration)

        @block.vector
        def _(dve):
            heads = lambda a, n: a.rearrange("p (h d) -> p h d", h=n)

            def newton(buf, v, n_in, act_sem, act_value, step_sem, base):
                y, a, c2 = buf[:, 1, :], buf[:, 2, :], buf[:, 3, :]
                dve.wait_ge(act_sem, act_value)
                dve.tensor_tensor(a, y, y, ALU.mult).then_inc(step_sem, 1)
                dve.wait_ge(step_sem, base + 1)
                dve.scalar_tensor_tensor(out=a, in0=v, scalar=EPS * n_in, in1=a, op0=ALU.add,
                                         op1=ALU.mult).then_inc(step_sem, 1)
                dve.wait_ge(step_sem, base + 2)
                dve.tensor_scalar(a, a, -0.5 / n_in, 1.5, ALU.mult, ALU.add).then_inc(step_sem, 1)
                dve.wait_ge(step_sem, base + 3)
                dve.tensor_tensor(c2, y, a, ALU.mult).then_inc(step_sem, 1)
                dve.wait_ge(step_sem, base + 4)

            def split_wq():
                wqh = wq_in[:, :, :].rearrange("p c (h d) -> p (c h) d", h=H)
                mean = lnq[:, 0, :]
                dve.wait_ge(wq_loaded, 16)
                dve.tensor_reduce(mean, wqh, AX.X, ALU.add).then_inc(wq_step, 1)
                dve.wait_ge(wq_step, 1)
                dve.tensor_scalar(mean, mean, 1.0 / HD, None, ALU.mult).then_inc(wq_step, 1)
                dve.wait_ge(wq_step, 2)
                dve.tensor_tensor(wqh, wqh, mean.unsqueeze(2).broadcast_to([P, C * H, HD]),
                                  ALU.subtract).then_inc(wq_step, 1)
                for c in range(C):
                    dve.wait_ge(wq_hi_done, c + 1)
                    dve.tensor_tensor(wq_lo[:, c, :].rearrange("p (i g d) -> p i g d", i=HC, g=G),
                                      by_place(wq_in[:, c, :]),
                                      wq_hi[:, c, :].rearrange("p (i g d) -> p i g d", i=HC, g=G).bitcast(F32),
                                      ALU.subtract).then_inc(wq_split, 1)

            kh = keys.rearrange("p b (h d) -> p (b h) d", h=H)
            kh2 = keys2.rearrange("p b (h d) -> p (b h) d", h=H)
            per_head = lambda a: a.unsqueeze(2).broadcast_to([P, NB * H, HD])
            on_heads = lambda a: a.unsqueeze(1).broadcast_to([P, NB * H, HD])

            def key_norm(part):
                if part == 0:
                    dve.wait_ge(keys_moved, NB)
                    dve.tensor_reduce(kst[:, 4, :], kh, AX.X, ALU.add).then_inc(key_step, 1)
                    dve.wait_ge(key_step, 1)
                    dve.tensor_scalar(kst[:, 4, :], kst[:, 4, :], 1.0 / HD, None, ALU.mult).then_inc(key_step, 1)
                    dve.wait_ge(key_step, 2)
                    dve.tensor_tensor(kh, kh, per_head(kst[:, 4, :]), ALU.subtract).then_inc(key_step, 1)
                elif part == 1:
                    dve.wait_ge(key_step, 3)
                    dve.tensor_tensor(kh2, kh, kh, ALU.mult).then_inc(key_step, 1)
                    dve.wait_ge(key_step, 4)
                    dve.tensor_reduce(kst[:, 5, :], kh2, AX.X, ALU.add).then_inc(key_step, 1)
                elif part == 2:
                    newton(kst, kst[:, 5, :], HD, key_guess, 2, key_step, 5)
                    dve.tensor_tensor(kh, kh, per_head(kst[:, 3, :]), ALU.mult).then_inc(key_step, 1)
                else:
                    dve.wait_ge(key_step, 10)
                    dve.wait_ge(params_loaded, PARAMS)
                    dve.tensor_tensor(kh, kh, on_heads(gk_row[:, :]), ALU.mult).then_inc(key_step, 1)
                    dve.wait_ge(key_step, 11)
                    for b in range(NB):
                        dve.tensor_tensor(keys2[:, b, :].rearrange("p (i g d) -> p i g d", i=HC, g=G),
                                          by_place(keys[:, b, :]),
                                          bk_row[:, :].unsqueeze(1).unsqueeze(1).broadcast_to([P, HC, G, HD]),
                                          ALU.add).then_inc(key_step, 1)

            def keys_low():
                for b in range(NB):
                    dve.wait_ge(keys_hi_done, b + 1)
                    dve.tensor_tensor(kn_lo[:, b, :], (AT, DEN)[b][:, :], kn_hi[:, b, :].bitcast(F32),
                                      ALU.subtract).then_inc(keys_split, 1)

            def aggregate(bn, mv, bn_sem, mv_sem, count):
                dve.wait_ge(bn_sem, count)
                dve.tensor_copy(spare[:, :], bn[:, 0, 0:1])
                for j in range(TB):
                    dve.bn_aggr(mv[:, j, :], bn[:, j, :]).then_inc(mv_sem, 1)

            def stats1(T, j):
                dve.wait_ge(x_loaded[j], T * 16 + 16)
                dve.bn_stats(bn1[:, j, :], xin[:, j, :]).then_inc(bn1_done, 1)

            def aggregate1(T):
                aggregate(bn1, mv1, bn1_done, mv1_done, T * TB + TB)

            def newton1(T):
                newton(ln1, mv1[:, :, 1], 1, ln1_act, T * 2 + 2, ln1_step, T * 4)

            def z1_norm(T, j):
                dve.tensor_scalar(xin[:, j, :], xin[:, j, :], mv1[:, j, 0:1], ln1[:, 3, j:j + 1],
                                  ALU.subtract, ALU.mult).then_inc(z1_done, 1)

            def z1_low(T, j):
                dve.wait_ge(zt_hi_done, T * TB + j + 1)
                dve.tensor_tensor(zt_lo[:, j % 2, :, :].rearrange("p c n -> p (c n)"), z1_bank[j][:, :],
                                  zt_hi[:, j % 2, :, :].rearrange("p c n -> p (c n)").bitcast(F32),
                                  ALU.subtract).then_inc(zt_lo_done, 1)

            def sum_squares(T, j):
                dve.wait_ge(sq_done, T * TB + j + 1)
                dve.tensor_reduce(ssq[:, j, :], heads(sq[:, :], H), AX.X, ALU.add).then_inc(ssq_done, 1)

            def newton_q(T):
                newton(lnq, ssq[:, :, :].rearrange("p j h -> p (j h)"), HD, lnq_act, T * 2 + 2, lnq_step, T * 4)

            def norm_q(T, j):
                uj = heads(u[:, j, :], H)
                dve.tensor_tensor(uj, uj, lnq[:, 3, j * H:(j + 1) * H].unsqueeze(2).broadcast_to([P, H, HD]),
                                  ALU.mult).then_inc(un_done, 1)

            def q_full(T, j):
                dve.wait_ge(qt_hi_done, T * TB + j + 1)
                dve.tensor_scalar(u[:, j, :], qt_bank[j][:, :], gq_col[:, 0:1], bq_col[:, 0:1], ALU.mult,
                                  ALU.add).then_inc(qf_done, 1)

            def row_max(T, gr, j):
                half, tile = gr // 2, gr % 2 * TB + j
                dve.wait_ge(maxs_done[half], T * MAX_TILES + tile + 1)
                if tile == 0 and not first(T):
                    dve.wait_ge(mx_turned[half], T)
                dve.tensor_reduce(mx[:, j, gr * HC:(gr + 1) * HC],
                                  maxs_bank[gr][j][:, :].rearrange("p (i n) -> p i n", i=HC), AX.X,
                                  ALU.max).then_inc(mx_done[half], 1)

            def reciprocal(t):
                dve.wait_ge(pv_done, t * PAIRS + PAIRS)
                dve.reciprocal(rden[:, :], DEN[:, :]).then_inc(rden_done, 1)

            def rden_low(t):
                dve.wait_ge(rden_hi_done, t + 1)
                dve.tensor_tensor(rden_lo[:, :], rden[:, :], rden_hi[:, :].bitcast(F32),
                                  ALU.subtract).then_inc(rden_lo_done, 1)

            def normalise(T, c):
                dve.wait_ge(spread_done, T * C + c + 1)
                dve.wait_ge(att_moved, T * C + c + 1)
                dve.tensor_tensor(att[:, c, :], spread_bank[c][:, :], att[:, c, :], ALU.mult).then_inc(att_done, 1)

            def residual1(T, j):
                dve.wait_ge(o_done, T * TB + j + 1)
                dve.wait_ge(xr_loaded[j], T * 16 + 16)
                dve.tensor_tensor(x1[:, j, :], o_bank[j][:, :], x1[:, j, :], ALU.add).then_inc(x1_done, 1)

            def stats2(T, j):
                dve.wait_ge(x1_done, T * TB + j + 1)
                dve.bn_stats(bn2[:, j, :], x1[:, j, :]).then_inc(bn2_done, 1)

            def aggregate2(T):
                aggregate(bn2, mv2, bn2_done, mv2_done, T * TB + TB)

            def newton2(T):
                newton(ln2, mv2[:, :, 1], 1, ln2_act, T * 2 + 2, ln2_step, T * 4)

            def z2_norm(T, j):
                if j >= 2:
                    dve.wait_ge(z2_turned, T * TB + j - 1)
                dve.tensor_scalar(z2[:, j % 2, :], x1[:, j, :], mv2[:, j, 0:1], ln2[:, 3, j:j + 1],
                                  ALU.subtract, ALU.mult).then_inc(z2_done, 1)

            def z2_low(T, j):
                cols = slice(j * P, (j + 1) * P)
                dve.wait_ge(z2t_hi_done, T * TB + j + 1)
                dve.tensor_tensor(z2t_lo[:, :, cols], z2_bank[j][:, :].rearrange("p (c n) -> p c n", c=C),
                                  z2t_hi[:, :, cols].bitcast(F32), ALU.subtract).then_inc(z2t_lo_done, 1)

            def residual2(T, j):
                dve.wait_ge(y_done, T * TB + j + 1)
                dve.wait_ge(bout_added, T * TB + j + 1)
                dve.tensor_tensor(x1[:, j, :], y_bank[j][:, :], x1[:, j, :], ALU.add).then_inc(out_done, 1)

            dve.wait_ge(consts, NCONSTS)
            dve.tensor_copy(bc_sel[:, :, :], bc_sel_f[:, :, :]).then_inc(wq_split, 1)
            dve.tensor_tensor(pair_eye, ident[:, 0:M], ident[:, M:2 * M], ALU.add).then_inc(wq_split, 1)
            split_wq()
            for j in range(TB):
                stats1(0, j)
            aggregate1(0)
            newton1(0)
            for j in range(TB):
                z1_norm(0, j)

            def iteration(t, kb, kf, g, f, a, b):
                N, F, B, prologue = t + 2, t + 1, t - 1, isinstance(t, int) and t == -1
                if f:
                    z1_low(F, 0)
                if b:
                    normalise(B, 0)
                if a:
                    row_max(t, 2, 0)
                    row_max(t, 2, 1)
                if f:
                    z1_low(F, 1)
                if prologue:
                    key_norm(0)
                if a:
                    row_max(t, 2, 2)
                if b:
                    normalise(B, 1)
                    normalise(B, 2)
                if f:
                    sum_squares(F, 0)
                    z1_low(F, 2)
                if b:
                    normalise(B, 3)
                if g:
                    stats1(N, 0)
                if a:
                    row_max(t, 2, 3)
                if f:
                    z1_low(F, 3)
                if prologue:
                    key_norm(1)
                if g:
                    stats1(N, 1)
                    stats1(N, 2)
                if f:
                    sum_squares(F, 1)
                if prologue:
                    key_norm(2)
                if g:
                    stats1(N, 3)
                if a:
                    row_max(t, 3, 0)
                if g:
                    aggregate1(N)
                if f:
                    sum_squares(F, 2)
                if prologue:
                    key_norm(3)
                if a:
                    row_max(t, 3, 1)
                    row_max(t, 3, 2)
                if f:
                    sum_squares(F, 3)
                if b:
                    residual1(B, 0)
                    stats2(B, 0)
                if f:
                    newton_q(F)
                    norm_q(F, 0)
                    norm_q(F, 1)
                if b:
                    residual1(B, 1)
                if a:
                    row_max(t, 3, 3)
                if f:
                    norm_q(F, 2)
                    norm_q(F, 3)
                if prologue:
                    keys_low()
                if b:
                    residual1(B, 2)
                    stats2(B, 1)
                    stats2(B, 2)
                if f:
                    q_full(F, 0)
                if b:
                    residual1(B, 3)
                    stats2(B, 3)
                    aggregate2(B)
                if f:
                    q_full(F, 1)
                if b:
                    newton2(B)
                    z2_norm(B, 0)
                    z2_norm(B, 1)
                if f:
                    q_full(F, 2)
                if b:
                    z2_norm(B, 2)
                    z2_norm(B, 3)
                    z2_low(B, 0)
                    z2_low(B, 1)
                    z2_low(B, 2)
                    z2_low(B, 3)
                if f:
                    q_full(F, 3)
                if g:
                    newton1(N)
                if f:
                    row_max(F, 0, 0)
                    row_max(F, 0, 1)
                    row_max(F, 0, 2)
                    row_max(F, 0, 3)
                    row_max(F, 1, 0)
                    row_max(F, 1, 1)
                if g:
                    z1_norm(N, 0)
                if b:
                    residual2(B, 0)
                    residual2(B, 1)
                    residual2(B, 2)
                if f:
                    row_max(F, 1, 2)
                    row_max(F, 1, 3)
                if g:
                    z1_norm(N, 1)
                if b:
                    residual2(B, 3)
                if a:
                    reciprocal(t)
                if g:
                    z1_norm(N, 2)
                    z1_norm(N, 3)
                if a:
                    rden_low(t)

            iterations(dve, iteration)

        @block.scalar
        def _(act):
            def rsqrt_guess(v, buf, n_in, in_sem, in_value, act_sem, act_value):
                act.wait_ge(in_sem, in_value)
                act.activation(buf[:, 0, :], v, ACT.Ln, bias=EPS, scale=1.0 / n_in).then_inc(act_sem, 1)
                act.wait_ge(act_sem, act_value - 1)
                act.activation(buf[:, 1, :], buf[:, 0, :], ACT.Exp, scale=-0.5).then_inc(act_sem, 1)

            def guess1(T):
                rsqrt_guess(mv1[:, :, 1], ln1, 1, mv1_done, T * TB + TB, ln1_act, T * 2 + 2)

            def guess2(T):
                rsqrt_guess(mv2[:, :, 1], ln2, 1, mv2_done, T * TB + TB, ln2_act, T * 2 + 2)

            def guess_q(T):
                rsqrt_guess(ssq[:, :, :].rearrange("p j h -> p (j h)"), lnq, HD, ssq_done, T * TB + TB,
                            lnq_act, T * 2 + 2)

            def z1_high(T, j):
                act.wait_ge(z1_turned, T * TB + j + 1)
                if j >= 2:
                    act.wait_ge(q_done, T * TB + j - 1)
                act.activation(zt_hi[:, j % 2, :, :].rearrange("p c n -> p (c n)"), z1_bank[j][:, :],
                               ACT.Copy).then_inc(zt_hi_done, 1)

            def move_u(T, j):
                act.wait_ge(q_done, T * TB + j + 1)
                if not first(T):
                    act.wait_ge(qt_lo_done, T * TB + j + 1 - TB)
                act.activation(u[:, j, :], q_bank[j][:, :], ACT.Copy).then_inc(u_done, 1)

            def q_high(T, j):
                act.wait_ge(q_turned, T * TB + j + 1)
                if j == 0 and not first(T):
                    for gr in range(G):
                        act.wait_ge(stacked[gr], T * 48)
                act.activation(qt_hi[:, :, j * P:(j + 1) * P], qt_bank[j][:, :].rearrange("p (i n) -> p i n", i=HC),
                               ACT.Identity, bias=bq_col[:, 0:1], scale=gq_col[:, 0:1]).then_inc(qt_hi_done, 1)

            def move_max(T, half):
                act.wait_ge(mx_turned[half], T + 1)
                if not first(T):
                    act.wait_ge(max_stacked[half], T * 16)
                act.activation(mxt[:, half, :], mxt_bank[half][0:H // 2, :], ACT.Copy).then_inc(mxt_done[half], 1)

            def exponential(t, h):
                act.wait_ge(scores_done, t * H + h + 1)
                if h >= PR or not first(t):
                    act.wait_ge(pv_done, t * PAIRS + (h - PR) // 2 + 1)
                act.activation(prob[:, h % PR, :], score_bank[h][:, :], ACT.Exp, scale=SCALE).then_inc(exp_done, 1)

            def move_att(t, c):
                act.wait_ge(pv_done, t * PAIRS + 2 * (c + 1))
                if not first(t):
                    act.wait_ge(at_lo_done, t * C + c + 1 - C)
                act.activation(att[:, c, :], AT[:, :], ACT.Copy).then_inc(att_moved, 1)

            def rden_high(t):
                act.wait_ge(rden_done, t + 1)
                if not first(t):
                    act.wait_ge(spread_done, t * C)
                act.activation(rden_hi[:, :], rden[:, :], ACT.Copy).then_inc(rden_hi_done, 1)

            def att_high(T, c):
                act.wait_ge(att_done, T * C + c + 1)
                act.activation(at_hi[:, c, :], att[:, c, :], ACT.Copy).then_inc(at_hi_done, 1)

            def z2_high(T, j):
                act.wait_ge(z2_turned, T * TB + j + 1)
                if j == 0:
                    act.wait_ge(o_done, T * TB + TB)
                act.activation(z2t_hi[:, :, j * P:(j + 1) * P], z2_bank[j][:, :].rearrange("p (c n) -> p c n", c=C),
                               ACT.Copy).then_inc(z2t_hi_done, 1)

            def move_s(T):
                act.wait_ge(s_mm_done, T + 1)
                act.activation(s_in[:, :], s_bank[:, :], ACT.Identity, bias=bin_col[:, 0:1]).then_inc(s_done, 1)

            def hidden(T, hh):
                act.wait_ge(s_done, T + 1)
                if hh >= RR:
                    act.wait_ge(hsum_done, T * HH + hh + 1 - RR)
                act.activation(hid[:, hh % RR, :], s_in[:, :], ACT.Relu, bias=b1_col[:, hh:hh + 1],
                               scale=w1_col[:, hh:hh + 1]).then_inc(hid_done, 1)

            def move_g(T):
                act.wait_ge(hsum_done, T * HH + HH)
                act.activation(g_mid[:, :], g_bank[:, :], ACT.Identity, bias=b2_col[:, 0:1]).then_inc(g_done, 1)

            act.preload_act_table_set("natural_log_exp_and_others")
            for b in range(NB):
                act.wait_ge(ctx_turned, b + 1)
                act.activation(ctx_t[:, b, :], (AT, DEN)[b][:, :], ACT.Copy).then_inc(ctx_moved, 1)
            act.wait_ge(kv_projected, 1)
            act.activation(keys[:, 0, :], AT[:, :], ACT.Copy).then_inc(keys_moved, 1)
            act.wait_ge(wq_step, 3)
            for c in range(C):
                act.activation(wq_hi[:, c, :].rearrange("p (i g d) -> p i g d", i=HC, g=G), by_place(wq_in[:, c, :]),
                               ACT.Copy).then_inc(wq_hi_done, 1)
            act.wait_ge(kv_projected, 2)
            act.activation(keys[:, 1, :], DEN[:, :], ACT.Copy).then_inc(keys_moved, 1)
            guess1(0)
            for b in range(NB):
                act.wait_ge(kv_projected, NB + b + 1)
                act.activation(v_kv[b][:, :], (AT, DEN)[b][:, :], ACT.Copy).then_inc(values_moved, 1)

            def split_weights():
                act.wait_ge(wo_loaded, 32)
                act.activation(wo_hi[:, :, :], wo_in[:, :, :], ACT.Copy).then_inc(wo_hi_done, 1)
                for half in range(2):
                    act.activation(win_hi[:, :, half, :], win_in, ACT.Copy).then_inc(wo_hi_done, 1)

            def iteration(t, kb, kf, g, f, a, b):
                N, F, B, prologue = t + 2, t + 1, t - 1, isinstance(t, int) and t == -1
                if isinstance(t, int) and t == 0:
                    split_weights()
                if f:
                    z1_high(F, 0)
                    z1_high(F, 1)
                if b:
                    att_high(B, 0)
                if f:
                    move_u(F, 0)
                    z1_high(F, 2)
                if b:
                    att_high(B, 1)
                if f:
                    move_u(F, 1)
                if b:
                    att_high(B, 2)
                    att_high(B, 3)
                if f:
                    z1_high(F, 3)
                if a:
                    exponential(t, 0)
                if f:
                    move_u(F, 2)
                if prologue:
                    rsqrt_guess(kst[:, 5, :], kst, HD, key_step, 5, key_guess, 2)
                if a:
                    exponential(t, 1)
                if f:
                    move_u(F, 3)
                    guess_q(F)
                if prologue:
                    for k in range(NB):
                        act.wait_ge(keys_turned, k + 1)
                        act.activation(kn_hi[:, k, :], (AT, DEN)[k][:, :], ACT.Copy).then_inc(keys_hi_done, 1)
                    act.wait_ge(params_loaded, PARAMS)
                if a:
                    exponential(t, 2)
                    exponential(t, 3)
                if f:
                    q_high(F, 0)
                if a:
                    move_max(t, 1)
                if f:
                    q_high(F, 1)
                if b:
                    guess2(B)
                if a:
                    exponential(t, 4)
                if f:
                    q_high(F, 2)
                if a:
                    exponential(t, 5)
                    move_att(t, 0)
                    exponential(t, 6)
                if b:
                    z2_high(B, 0)
                    z2_high(B, 1)
                if a:
                    exponential(t, 7)
                if b:
                    z2_high(B, 2)
                    z2_high(B, 3)
                if a:
                    exponential(t, 8)
                if f:
                    q_high(F, 3)
                if a:
                    exponential(t, 9)
                    move_att(t, 1)
                if g:
                    guess1(N)
                if a:
                    exponential(t, 10)
                    exponential(t, 11)
                if b:
                    move_s(B)
                    hidden(B, 0)
                    hidden(B, 1)
                    hidden(B, 2)
                    hidden(B, 3)
                    hidden(B, 4)
                    hidden(B, 5)
                    hidden(B, 6)
                    hidden(B, 7)
                if a:
                    exponential(t, 12)
                if b:
                    move_g(B)
                if a:
                    exponential(t, 13)
                    move_att(t, 2)
                    exponential(t, 14)
                    exponential(t, 15)
                    move_att(t, 3)
                if f:
                    move_max(F, 0)
                if a:
                    rden_high(t)

            iterations(act, iteration)

        @block.tensor
        def _(pe):
            def last_user(*users):
                for there, semaphore, value in users:
                    if there:
                        pe.wait_ge(semaphore, value)
                        return

            def three_pass(dst, pairs):
                terms = [t for (lh, ll, rh, rl) in pairs for t in ((lh, rh), (lh, rl), (ll, rh))]
                for n, (l, r) in enumerate(terms):
                    ins = pe.matmul(dst, l, r, start=n == 0, stop=n == len(terms) - 1)
                return ins

            def turn(dst, src, done):
                for n in range(4):
                    ins = pe.transpose(dst[:, n * P:(n + 1) * P], src(n), ident[:, :])
                ins.then_inc(done, 1)

            columns = lambda a: lambda n: a[:, n * P:(n + 1) * P]

            pe.wait_ge(consts, NCONSTS)
            pe.wait_ge(kv_loaded, 32)
            for b in range(NB):
                turn((AT, DEN)[b], columns(ctx_in[:, b, :]), ctx_turned)
            for n, w in enumerate((wk_in, wv_in)):
                for b in range(NB):
                    if n == 0:
                        pe.wait_ge(ctx_moved, NB)
                    else:
                        pe.wait_ge(keys_moved, b + 1)
                        pe.wait_ge(wv_loaded, 16)
                    for c in range(C):
                        ins = pe.matmul((AT, DEN)[b][:, :], ctx_t[:, b, c * P:(c + 1) * P], w[:, c, :], start=c == 0,
                                        stop=c == C - 1)
                    ins.then_inc(kv_projected, 1)

            def turn_z1(T, j):
                pe.wait_ge(z1_done, T * TB + j + 1)
                turn(z1_bank[j], columns(xin[:, j, :]), z1_turned)

            def project_q(T, j):
                pe.wait_ge(zt_lo_done, T * TB + j + 1)
                three_pass(q_bank[j][:, :], [(zt_hi[:, j % 2, c, :], zt_lo[:, j % 2, c, :], wq_hi[:, c, :], wq_lo[:, c, :])
                                             for c in range(C)]).then_inc(q_done, 1)

            def turn_keys():
                pe.wait_ge(key_step, 13)
                pe.wait_ge(values_moved, NB)
                for b in range(NB):
                    turn((AT, DEN)[b], columns(keys2[:, b, :]), keys_turned)
    
            def turn_q(T, j):
                pe.wait_ge(un_done, T * TB + j + 1)
                turn(qt_bank[j], columns(u[:, j, :]), q_turned)

            def max_scores(T, kb, gr, j):
                if j == 0:
                    pe.wait_ge(stacked[gr], T * 48 + 48)
                for i in range(HC):
                    h = gr * HC + i
                    ins = pe.matmul(maxs_bank[gr][j][:, i * KV:(i + 1) * KV], q_stack[0:3 * HD, h, j * P:(j + 1) * P],
                                    k_stack[kb][0:3 * HD, h, :], start=True, stop=True)
                ins.then_inc(maxs_done[gr // 2], 1)

            def turn_max(T, half):
                pe.wait_ge(mx_done[half], (T + 1) * MAX_TILES)
                for j in range(TB):
                    ins = pe.transpose(mxt_bank[half][0:H // 2, j * P:(j + 1) * P],
                                       mx[:, j, H // 2 * half:H // 2 * (half + 1)], ident[:, :])
                ins.then_inc(mx_turned[half], 1)

            def scores(t, kb, h):
                if h % (H // 2) == 0:
                    pe.wait_ge(max_stacked[h // (H // 2)], t * 16 + 16)
                pe.matmul(score_bank[h][:, :], k_stack[kb][0:3 * HD + 1, h, :], q_stack[0:3 * HD + 1, h, :],
                          start=True, stop=True).then_inc(scores_done, 1)

            def values(t, kb, pair):
                c, h = pair // 2, 2 * pair
                pe.wait_ge(exp_done, t * H + h + 2)
                if pair % 2 == 0 and not (first(t) and c == 0):
                    pe.wait_ge(att_moved, t * C + c)
                if pair == 0 and not first(t):
                    pe.wait_ge(rden_done, t)
                rows = lambda n: slice(HD * (n % HC), HD * (n % HC + 1))
                for n in (h, h + 1):
                    pe.matmul(AT[rows(n), :], v_kv[kb][:, n * HD:(n + 1) * HD], prob[:, n % PR, :], start=True,
                              stop=True)
                for n in (h, h + 1):
                    ins = pe.matmul(DEN[rows(n + 2), :], den_sel[:, c, :], prob[:, n % PR, :], start=c == 0,
                                    stop=c == C - 1)
                ins.then_inc(pv_done, 1)

            def spread(T, c):
                if c == 0:
                    pe.wait_ge(rden_lo_done, T + 1)
                pe.matmul(spread_bank[c][:, :], bc_sel[:, c, :], rden_hi[:, :], start=True, stop=False)
                pe.matmul(spread_bank[c][:, :], bc_sel[:, c, :], rden_lo[:, :], start=False, stop=True).then_inc(spread_done, 1)

            def project_o(T, j):
                cols = slice(j * P, (j + 1) * P)
                if j == 0:
                    pe.wait_ge(at_lo_done, T * C + C)
                three_pass(o_bank[j][:, :], [(at_hi[:, c, cols], at_lo[:, c, cols], wo_hi[:, c, :], wo_lo[:, c, :])
                                             for c in range(C)]).then_inc(o_done, 1)

            def turn_z2(T, j):
                pe.wait_ge(z2_done, T * TB + j + 1)
                turn(z2_bank[j], columns(z2[:, j % 2, :]), z2_turned)

            def project_s(T):
                pe.wait_ge(z2t_lo_done, T * TB + TB)
                both = lambda w, c: w[:, c, :, :].rearrange("p a m -> p (a m)")
                three_pass(s_bank[:, :], [(both(win_hi, c), both(win_lo, c), z2t_hi[:, c, :], z2t_lo[:, c, :])
                                         for c in range(C)]).then_inc(s_mm_done, 1)

            def sum_hidden(T, hh):
                half = hh % 2
                pe.wait_ge(hid_done, T * HH + hh + 1)
                pe.matmul(g_bank[M * half:M * (half + 1), :], w2_diag[:, hh, :], hid[:, hh % RR, :],
                          start=hh < 2, stop=hh >= HH - 2).then_inc(hsum_done, 1)

            def project_y(T, j):
                if j == 0:
                    pe.wait_ge(g_done, T + 1)
                pe.matmul(y_bank[j][:, :], g_mid[:, j * P:(j + 1) * P], wout2[:, :], start=True, stop=True).then_inc(y_done, 1)

            def iteration(t, kb, kf, g, f, a, b):
                F, B, prologue = t + 1, t - 1, isinstance(t, int) and t == -1
                f_before = not isinstance(t, int) or 0 <= t < BLOCKS
                a_before = not isinstance(t, int) or 1 <= t <= BLOCKS
                b_before = not isinstance(t, int) or t >= 2
                if a:
                    last_user((f_before, mxt_done[0], t + 1), (b_before, out_done, (t - 2) * TB + 4),
                              (a_before, exp_done, (t - 1) * H + 9))
                    max_scores(t, kb, 2, 0)
                if f:
                    last_user((a_before, exp_done, (t - 1) * H + 15), (b_before, z2t_lo_done, (t - 2) * TB + 4),
                              (f_before, qf_done, t * TB + 3))
                    turn_z1(F, 0)
                if a:
                    last_user((f_before, mx_done[0], t * MAX_TILES + 8), (b_before, out_done, (t - 2) * TB + 2),
                              (a_before, exp_done, (t - 1) * H + 12))
                    max_scores(t, kb, 2, 1)
                if f:
                    last_user((a_before, exp_done, (t - 1) * H + 14), (b_before, z2t_lo_done, (t - 2) * TB + 2),
                              (f_before, qf_done, t * TB + 2))
                    turn_z1(F, 1)
                if a:
                    last_user((a_before, exp_done, (t - 1) * H + 16), (f_before, mx_done[0], t * MAX_TILES + 5),
                              (b_before, att_done, (t - 2) * C + 4))
                    max_scores(t, kb, 2, 2)
                if b:
                    last_user((f_before, mx_done[0], t * MAX_TILES + 7), (a_before, exp_done, (t - 1) * H + 11),
                              (b_before, z2t_lo_done, (t - 2) * TB + 3))
                    spread(B, 0)
                if f:
                    pe.wait_ge(zt_lo_done, F * TB + 1)
                    project_q(F, 0)
                if b:
                    last_user((a, mx_done[1], t * MAX_TILES + 2), (f_before, mx_done[0], t * MAX_TILES + 8),
                              (b_before, out_done, (t - 2) * TB + 2), (a_before, exp_done, (t - 1) * H + 12))
                    spread(B, 1)
                    pe.wait_ge(att_done, B * C + 1)
                    spread(B, 2)
                if a:
                    pe.wait_ge(mx_done[1], t * MAX_TILES + 1)
                    scores(t, kb, 0)
                if f:
                    pe.wait_ge(u_done, F * TB + 1)
                    turn_z1(F, 2)
                    last_user((b, att_done, B * C + 2), (a, mx_done[1], t * MAX_TILES + 2),
                              (f_before, mx_done[0], t * MAX_TILES + 8), (b_before, out_done, (t - 2) * TB + 2),
                              (a_before, exp_done, (t - 1) * H + 12))
                    project_q(F, 1)
                if b:
                    last_user((a, mx_done[1], t * MAX_TILES + 3), (a_before, exp_done, (t - 1) * H + 16),
                              (f_before, mx_done[0], t * MAX_TILES + 5), (b_before, att_done, (t - 2) * C + 4))
                    spread(B, 3)
                if f:
                    pe.wait_ge(zt_lo_done, F * TB + 2)
                    turn_z1(F, 3)
                if a:
                    last_user((b, att_done, B * C + 3), (f_before, mx_done[0], t * MAX_TILES + 7),
                              (a_before, exp_done, (t - 1) * H + 11), (b_before, z2t_lo_done, (t - 2) * TB + 3))
                    max_scores(t, kb, 2, 3)
                if f:
                    pe.wait_ge(u_done, F * TB + 2)
                    project_q(F, 2)
                if a:
                    last_user((b, att_done, B * C + 4), (a, mx_done[1], t * MAX_TILES + 3))
                    scores(t, kb, 1)
                    pe.wait_ge(mx_done[1], t * MAX_TILES + 4)
                    max_scores(t, kb, 3, 0)
                if f:
                    pe.wait_ge(zt_lo_done, F * TB + 3)
                    project_q(F, 3)
                if prologue:
                    turn_keys()
                if a:
                    pe.wait_ge(exp_done, t * H + 1)
                    max_scores(t, kb, 3, 1)
                    last_user((f, u_done, F * TB + 3), (b, att_done, B * C + 2), (a, mx_done[1], t * MAX_TILES + 2))
                    max_scores(t, kb, 3, 2)
                if b:
                    last_user((f, zt_lo_done, F * TB + 4), (a_before, exp_done, (t - 1) * H + 14),
                              (b_before, z2t_lo_done, (t - 2) * TB + 2), (f_before, qf_done, t * TB + 2))
                    project_o(B, 0)
                    last_user((f, u_done, F * TB + 4), (a_before, exp_done, (t - 1) * H + 15),
                              (b_before, z2t_lo_done, (t - 2) * TB + 4), (f_before, qf_done, t * TB + 3))
                    project_o(B, 1)
                if a:
                    last_user((b, x1_done, B * TB + 1), (f, zt_lo_done, F * TB + 4),
                              (a_before, exp_done, (t - 1) * H + 14), (b_before, z2t_lo_done, (t - 2) * TB + 2),
                              (f_before, qf_done, t * TB + 2))
                    scores(t, kb, 2)
                    pe.wait_ge(mx_done[1], t * MAX_TILES + 7)
                    max_scores(t, kb, 3, 3)
                    pe.wait_ge(mx_done[1], t * MAX_TILES + 6)
                    scores(t, kb, 3)
                if b:
                    last_user((a, mx_done[1], t * MAX_TILES + 5), (b, att_done, B * C + 3))
                    project_o(B, 2)
                if f:
                    last_user((a, mx_done[1], t * MAX_TILES + 8), (f, u_done, F * TB + 3))
                    turn_q(F, 0)
                if b:
                    pe.wait_ge(x1_done, B * TB + 2)
                    project_o(B, 3)
                if a:
                    last_user((b, x1_done, B * TB + 3), (a, mx_done[1], t * MAX_TILES + 5))
                    turn_max(t, 1)
                if f:
                    last_user((a, exp_done, t * H + 3), (b, x1_done, B * TB + 1), (f, zt_lo_done, F * TB + 4))
                    turn_q(F, 1)
                if a:
                    pe.wait_ge(exp_done, t * H + 2)
                    scores(t, kb, 4)
                    values(t, kb, 0)
                    last_user((f, qf_done, F * TB + 1), (a, mx_done[1], t * MAX_TILES + 8))
                    scores(t, kb, 5)
                if f:
                    last_user((b, x1_done, B * TB + 4), (f, u_done, F * TB + 4))
                    turn_q(F, 2)
                if a:
                    values(t, kb, 1)
                if f:
                    last_user((a, exp_done, t * H + 5), (b, att_done, B * C + 4),
                              (a_before, exp_done, (t - 1) * H + 16), (f_before, mx_done[0], t * MAX_TILES + 5))
                    turn_q(F, 3)
                if prologue:
                    pe.wait_ge(keys_stacked, 16 * NB * G * 3)
                if a:
                    pe.wait_ge(mxt_done[1], t + 1)
                    scores(t, kb, 6)
                    pe.wait_ge(exp_done, t * H + 4)
                    scores(t, kb, 7)
                if b:
                    last_user((a, exp_done, t * H + 6), (f, qf_done, F * TB + 1), (b, att_done, B * C + 2))
                    turn_z2(B, 0)
                    last_user((f, qf_done, F * TB + 2), (a, exp_done, t * H + 3), (b, x1_done, B * TB + 1))
                    turn_z2(B, 1)
                if a:
                    values(t, kb, 2)
                if b:
                    last_user((a, exp_done, t * H + 7), (b, x1_done, B * TB + 3))
                    turn_z2(B, 2)
                    last_user((f, qf_done, F * TB + 3), (b, x1_done, B * TB + 4))
                    turn_z2(B, 3)
                if a:
                    pe.wait_ge(exp_done, t * H + 8)
                    scores(t, kb, 8)
                    values(t, kb, 3)
                    last_user((b, z2t_lo_done, B * TB + 2), (f, qf_done, F * TB + 2), (a, exp_done, t * H + 3))
                    scores(t, kb, 9)
                    last_user((b, z2t_lo_done, B * TB + 3), (a, exp_done, t * H + 7))
                    scores(t, kb, 10)
                    last_user((b, z2t_lo_done, B * TB + 1), (a, exp_done, t * H + 6))
                    scores(t, kb, 11)
                if b:
                    last_user((a, exp_done, t * H + 9), (f_before, mxt_done[0], t + 1),
                              (b_before, out_done, (t - 2) * TB + 4))
                    project_s(B)
                if a:
                    values(t, kb, 4)
                    last_user((b, z2t_lo_done, B * TB + 4), (f, qf_done, F * TB + 3),
                              (a_before, exp_done, (t - 1) * H + 15))
                    scores(t, kb, 12)
                    values(t, kb, 5)
                if b:
                    pe.wait_ge(s_done, B + 1)
                    sum_hidden(B, 0)
                    sum_hidden(B, 1)
                if a:
                    pe.wait_ge(exp_done, t * H + 10)
                    scores(t, kb, 13)
                if b:
                    sum_hidden(B, 2)
                if f:
                    last_user((a, exp_done, t * H + 12), (b, z2t_lo_done, B * TB + 1), (f, qf_done, F * TB + 1))
                    max_scores(F, kf, 0, 0)
                if b:
                    sum_hidden(B, 3)
                if f:
                    last_user((a, exp_done, t * H + 11), (b, z2t_lo_done, B * TB + 3),
                              (f_before, mx_done[0], t * MAX_TILES + 7))
                    max_scores(F, kf, 0, 1)
                if b:
                    sum_hidden(B, 4)
                if f:
                    pe.wait_ge(qf_done, F * TB + 4)
                    max_scores(F, kf, 0, 2)
                    pe.wait_ge(mx_done[0], F * MAX_TILES + 1)
                    max_scores(F, kf, 0, 3)
                if b:
                    sum_hidden(B, 5)
                    sum_hidden(B, 6)
                if f:
                    pe.wait_ge(mx_done[0], F * MAX_TILES + 3)
                    max_scores(F, kf, 1, 0)
                if b:
                    sum_hidden(B, 7)
                if f:
                    pe.wait_ge(mx_done[0], F * MAX_TILES + 4)
                    max_scores(F, kf, 1, 1)
                if a:
                    pe.wait_ge(exp_done, t * H + 13)
                    scores(t, kb, 14)
                    last_user((f, mx_done[0], F * MAX_TILES + 5), (a, exp_done, t * H + 5))
                    scores(t, kb, 15)
                if f:
                    pe.wait_ge(mx_done[0], F * MAX_TILES + 2)
                    max_scores(F, kf, 1, 2)
                if b:
                    pe.wait_ge(g_done, B + 1)
                    project_y(B, 0)
                    last_user((f, mx_done[0], F * MAX_TILES + 6), (a, exp_done, t * H + 12),
                              (b, z2t_lo_done, B * TB + 1))
                    project_y(B, 1)
                    pe.wait_ge(out_done, B * TB + 1)
                    project_y(B, 2)
                if a:
                    values(t, kb, 6)
                if f:
                    last_user((b, out_done, B * TB + 2), (f, mx_done[0], F * MAX_TILES + 6))
                    max_scores(F, kf, 1, 3)
                if b:
                    pe.wait_ge(out_done, B * TB + 3)
                    project_y(B, 3)
                if a:
                    values(t, kb, 7)
                if f:
                    last_user((b, out_done, B * TB + 4), (a, exp_done, t * H + 9), (f_before, mxt_done[0], t + 1))
                    turn_max(F, 0)

            def enter():
                pe.wait_ge(weights_split, WEIGHTS)
                pe.wait_ge(params_loaded, PARAMS)

            iterations(pe, iteration, enter)


_INS = ['x', 'ctx_1024', 'L0_xattn_Wq', 'L0_xattn_Wk', 'L0_xattn_Wv', 'L0_xattn_Wo', 'L0_xattn_gq', 'L0_xattn_bq',
        'L0_xattn_gk', 'L0_xattn_bk', 'L0_ffn_Win', 'L0_ffn_bin_', 'L0_ffn_W1', 'L0_ffn_b1', 'L0_ffn_W2',
        'L0_ffn_b2', 'L0_ffn_Wout', 'L0_ffn_bout']


def kernel(**inputs):
    import numpy as _np
    import concourse.bacc as _bacc
    from concourse import mybir as _mybir
    from concourse.bass_utils import run_bass_kernel_spmd as _run

    nc = _bacc.Bacc("TRN2", target_bir_lowering=False, num_devices=1)
    arrays, args = {}, []
    for name in _INS:
        a = _np.ascontiguousarray(inputs[name])
        arrays[f"in_{name}_dram"] = a
        args.append(nc.dram_tensor(f"in_{name}_dram", a.shape, _mybir.dt.from_np(a.dtype), kind="ExternalInput").ap())
    args.append(nc.dram_tensor("out_0_dram", inputs['x'].shape, _mybir.dt.float32, kind="ExternalOutput").ap())
    build_program(nc, *args)
    r = _run(nc, [arrays], core_ids=[0])
    return r.results[0]["out_0_dram"]
```

```python
import concourse.bass as bass
from concourse import mybir
from contextlib import ExitStack

F32 = mybir.dt.float32
F32R = mybir.dt.float32r
ALU = mybir.AluOpType
ACT = mybir.ActivationFunctionType
AX = mybir.AxisListType

P = 128
D = 512
C = D // P
H = 16
HD = D // H
HC = H // C
NB = 2
SQ = 2048
KV = 128
TB = 4
TOK = TB * P
BLOCKS = NB * SQ // TOK
M = 64
INNER = 16
HH = INNER // 2
EPS = 1e-5
SCALE = HD ** -0.5
PR = 4
RR = 4
G = H // HC
PAIRS = H // 2
MAX_TILES = HC // 2 * TB
NEYES = 4
NCONSTS = 3 + C + NB


def build_program(nc, x, ctx_kv, Wq, Wk, Wv, Wo, gq, bq, gk, bk, Win, bin_, W1, b1, W2, b2, Wout, bout, out):
    with ExitStack() as stack:
        def sb(name, shape, dt=F32):
            return stack.enter_context(nc.sbuf_tensor(name, shape, dt))

        def bank(name):
            return stack.enter_context(nc.psum_tensor(name, [P, D], F32))

        def sem(name):
            return stack.enter_context(nc.semaphore(name))

        wq_hi = sb("wq_hi", [P, C, D], F32R)
        wq_lo = sb("wq_lo", [P, C, D], F32R)
        wo_hi = sb("wo_hi", [P, C, D], F32R)
        wo_lo = sb("wo_lo", [P, C, D], F32R)
        win_hi = sb("win_hi", [P, C, 2, M], F32R)
        win_lo = sb("win_lo", [P, C, 2, M], F32R)
        wout_hi = sb("wout_hi", [P, D], F32R)
        wout_lo = sb("wout_lo", [P, D], F32R)
        w2_diag = sb("w2_diag", [P, HH, M])
        bout_row = sb("bout_row", [P, D])
        k_stack = [sb(f"k_stack{b}", [P, H, KV], F32R) for b in range(NB)]
        v_kv = [sb(f"v_kv{b}", [P, D]) for b in range(NB)]
        gq_col = sb("gq_col", [P, 1])
        bq_col = sb("bq_col", [P, 1])
        gk_row = sb("gk_row", [P, HD])
        bk_row = sb("bk_row", [P, HD])
        bin_col = sb("bin_col", [P, 1])
        w1_col = sb("w1_col", [P, HH])
        b1_col = sb("b1_col", [P, HH])
        w2_col = sb("w2_col", [P, HH])
        b2_col = sb("b2_col", [P, 1])
        ident = sb("ident", [P, P])
        den_sel = sb("den_sel", [P, C, HD])
        bc_sel = sb("bc_sel", [P, C, P], F32R)
        xin = sb("xin", [P, TB, D])
        zt_hi = sb("zt_hi", [P, 2, C, P], F32R)
        zt_lo = sb("zt_lo", [P, 2, C, P], F32R)
        u = sb("u", [P, TB, D])
        qt_hi = sb("qt_hi", [P, HC, TOK], F32R)
        qt_lo = sb("qt_lo", [P, HC, TOK], F32R)
        q_stack = sb("q_stack", [P, H, TOK], F32R)
        mx = sb("mx", [P, TB, H])
        mxt = sb("mxt", [H, TOK], F32R)
        k_diag = sb("k_diag", [P, HC, D], F32R)
        prob = sb("prob", [P, PR, TOK])
        att = sb("att", [P, C, TOK])
        at_hi = sb("at_hi", [P, C, TOK], F32R)
        at_lo = sb("at_lo", [P, C, TOK], F32R)
        rden = sb("rden", [P, TOK])
        sq = rden[:, :]
        bc_sel_f = rden[:, :].rearrange("p (c n) -> p c n", c=C)
        rden_hi, rden_lo = at_hi[:, C - 1, :], at_lo[:, C - 1, :]
        x1 = sb("x1", [P, TB, D])
        z2 = sb("z2", [P, 2, D])
        z2t_hi, z2t_lo = at_hi, at_lo
        s_in = sb("s_in", [P, TOK])
        win_in = s_in[:, 0:C * M].rearrange("p (c m) -> p c m", c=C)
        pair_eye = s_in[:, C * M:(C + 1) * M]
        kst = s_in[:, (C + 1) * M:].rearrange("p (k h) -> p k h", k=6)
        hid = sb("hid", [P, RR, TOK])
        g_hi, g_lo = at_hi[:, 0, :], at_lo[:, 0, :]
        bn1 = sb("bn1", [P, TB, 6])
        mv1 = sb("mv1", [P, TB, 2])
        bn2 = sb("bn2", [P, TB, 6])
        mv2 = sb("mv2", [P, TB, 2])
        ssq = sb("ssq", [P, TB, H])
        ln1 = sb("ln1", [P, 4, TB])
        ln2 = sb("ln2", [P, 4, TB])
        spare = sb("spare", [P, 1])
        lnq = sb("lnq", [P, 4, TB * H])

        AT = bank("AT")
        DEN = bank("DEN")
        banks = [bank(f"bank{n}") for n in range(6)]
        z1_bank = [banks[n] for n in (1, 4, 0, 3)]
        q_bank = [banks[n] for n in (1, 4, 2, 4)]
        qt_bank = [banks[n] for n in (0, 4, 5, 3)]
        maxs_bank = [[banks[n] for n in (3, 0, 2, 1)],
                     [banks[n] for n in (4, 3, 2, 0)],
                     [banks[n] for n in (5, 2, 1, 5)],
                     [banks[n] for n in (0, 3, 5, 1)]]
        mxt_bank = banks[5]
        score_bank = [banks[n] for n in (4, 0, 3, 2, 3, 5, 4, 1, 3, 5, 1, 2, 2, 3, 2, 1)]
        spread_bank = [banks[n] for n in (3, 2, 4, 5)]
        o_bank = [banks[n] for n in (0, 1, 2, 1)]
        z2_bank = [banks[n] for n in (3, 5, 1, 0)]
        s_bank, g_bank = banks[0], banks[0]
        y_bank = [banks[n] for n in (2, 0, 2, 0)]
        value_bank = [banks[n] for n in (0, 1)]

        names = """eyes consts params_loaded ctx_loaded wk_loaded wv_loaded wo_loaded ctx_turned ctx_moved kv_projected
            keys_moved values_moved wq_step wq_hi_done wq_split wo_hi_done weights_split key_step key_guess
            keys_turned keys_hi_done keys_split keys_stacked bn1_done mv1_done ln1_act ln1_step z1_done
            z1_turned zt_hi_done zt_lo_done q_done u_done sq_done ssq_done lnq_act lnq_step un_done q_turned
            qt_hi_done qf_done qt_lo_done scores_done exp_done pv_done att_moved rden_done rden_hi_done
            rden_lo_done spread_done att_done at_hi_done at_lo_done o_done x1_done bn2_done mv2_done ln2_act
            ln2_step z2_done bout_added z2_turned z2t_hi_done z2t_lo_done s_mm_done s_done hid_done hsum_done
            g_done y_done out_done mx_turned mxt_done k_diag_done g_hi_done wout_loaded odd_step odd_hidden""".split()
        sems = {name: sem(name) for name in names}
        (eyes, consts, params_loaded, ctx_loaded, wk_loaded, wv_loaded, wo_loaded, ctx_turned, ctx_moved,
         kv_projected, keys_moved, values_moved, wq_step, wq_hi_done, wq_split, wo_hi_done, weights_split,
         key_step, key_guess, keys_turned, keys_hi_done, keys_split, keys_stacked, bn1_done, mv1_done, ln1_act,
         ln1_step, z1_done, z1_turned, zt_hi_done, zt_lo_done, q_done, u_done, sq_done, ssq_done, lnq_act,
         lnq_step, un_done, q_turned, qt_hi_done, qf_done, qt_lo_done, scores_done, exp_done, pv_done, att_moved,
         rden_done, rden_hi_done, rden_lo_done, spread_done, att_done, at_hi_done, at_lo_done, o_done, x1_done,
         bn2_done, mv2_done, ln2_act, ln2_step, z2_done, bout_added, z2_turned, z2t_hi_done, z2t_lo_done,
         s_mm_done, s_done, hid_done, hsum_done, g_done, y_done, out_done, mx_turned, mxt_done, k_diag_done,
         g_hi_done, wout_loaded, odd_step, odd_hidden) = (sems[name] for name in names)
        x_loaded = [sem(f"x_loaded{j}") for j in range(TB)]
        xr_loaded = [sem(f"xr_loaded{j}") for j in range(TB)]
        wq_loaded = [sem(f"wq_loaded{c}") for c in range(C)]
        stored = [sem(f"stored{j}") for j in range(TB)]
        stacked = [sem(f"stacked{g}") for g in range(G)]
        maxs_done, mx_done, max_stacked = (
            [sem(f"{name}{half}") for half in range(2)] for name in ("maxs_done", "mx_done", "max_stacked"))

        PARAMS = 16 * (2 * HC + 4 + 8)
        WEIGHTS = 1 + 2 + 1 + HH

        block = stack.enter_context(nc.Block())

        x_t = x.rearrange("b (n j p) d -> (b n) j p d", p=P, j=TB)
        out_t = out.rearrange("b (n j p) d -> (b n) j p d", p=P, j=TB)

        wk_in, wv_in, wq_in, wo_in = att, hid, x1, x1
        ctx_in, keys = prob[:, 0:NB, :], prob[:, NB:2 * NB, :]
        ctx_t, wout_in, keys2 = z2, z2[:, 0, :], att[:, 0:NB, :]
        kn_hi, kn_lo = at_hi[:, 0:NB, :], at_lo[:, 0:NB, :]

        def iterations(engine, iteration, last, enter=lambda: None):
            per = BLOCKS // NB
            iteration(-1, 0, 0, g=True, f=True, a=False, b=False)
            iteration(0, 0, 0, g=True, f=True, a=True, b=False)
            enter()
            with engine.Fori(1, per - 1) as t:
                iteration(t, 0, 0, g=True, f=True, a=True, b=True)
            iteration(per - 1, 0, 1, g=True, f=True, a=True, b=True)
            with engine.Fori(per, BLOCKS - 2) as t:
                iteration(t, 1, 1, g=True, f=True, a=True, b=True)
            iteration(BLOCKS - 2, 1, 1, g=False, f=True, a=True, b=True)
            iteration(BLOCKS - 1, 1, 1, g=False, f=False, a=True, b=True)
            last(BLOCKS - 1)

        def by_place(a):
            return a.rearrange("p (g i d) -> p i g d", g=G, i=HC)

        def first(t):
            return isinstance(t, int) and t <= 0

        @block.sync
        def _(sp):
            for j in range(TB):
                sp.dma_start(xin[:, j, :], x_t[0, j]).then_inc(x_loaded[j], 16)
            sp.dma_start(ctx_in, ctx_kv.rearrange("b k d -> k b d")).then_inc(ctx_loaded, 16)
            for c in range(C):
                sp.dma_start(wq_in[:, c, :], Wq[c * P:(c + 1) * P, :]).then_inc(wq_loaded[c], 16)
            sp.dma_start(wk_in[:, :, :], Wk.rearrange("(c p) n -> p c n", p=P)).then_inc(wk_loaded, 16)
            sp.dma_start(wv_in[:, :, :], Wv.rearrange("(c p) n -> p c n", p=P)).then_inc(wv_loaded, 16)
            column = lambda a: a.rearrange("(p o) -> p o", o=1)
            row = lambda a, n: a.rearrange("(o n) -> o n", o=1).broadcast_to([P, n])
            for i in range(HC):
                rows = slice(HD * i, HD * (i + 1))
                sp.dma_start(gq_col[rows, :], column(gq)).then_inc(params_loaded, 16)
                sp.dma_start(bq_col[rows, :], column(bq)).then_inc(params_loaded, 16)
            sp.dma_start(gk_row[:, :], row(gk, HD)).then_inc(params_loaded, 16)
            sp.dma_start(bk_row[:, :], row(bk, HD)).then_inc(params_loaded, 16)
            sp.dma_start(bout_row[:, :], row(bout, D)).then_inc(params_loaded, 16)
            sp.wait_ge(eyes, NEYES)
            sp.dma_start(b2_col[0:M, :], column(b2)).then_inc(params_loaded, 16)
            for half in range(2):
                rows, units = slice(M * half, M * (half + 1)), slice(HH * half, HH * (half + 1))
                sp.dma_start(bin_col[rows, :], column(bin_)).then_inc(params_loaded, 16)
                sp.dma_start(w1_col[rows, :], W1[:, units]).then_inc(params_loaded, 16)
                sp.dma_start(b1_col[rows, :], b1[:, units]).then_inc(params_loaded, 16)
                sp.dma_start(w2_col[rows, :], W2[:, units]).then_inc(params_loaded, 16)
            sp.wait_ge(wq_split, 2 + C)
            sp.dma_start(wo_in[:, :, :], Wo.rearrange("(c p) n -> p c n", p=P)).then_inc(wo_loaded, 16)
            sp.dma_start(win_in, Win.rearrange("(c p) m -> p c m", p=P)).then_inc(wo_loaded, 16)

            def stack_keys(b):
                sp.wait_ge(keys_split, b + 1)
                for gr in range(G):
                    rows, heads = slice(HD * gr, HD * (gr + 1)), slice(HC * gr, HC * (gr + 1))
                    for part, src in enumerate((kn_hi, kn_hi, kn_lo)):
                        sp.dma_start(k_stack[b][HD * part:HD * (part + 1), heads, :].bitcast(F32),
                                     src[rows, b, :].rearrange("p (i n) -> p i n", i=HC).bitcast(F32)
                                     ).then_inc(keys_stacked, 16)

            def load_wout():
                sp.wait_ge(kv_projected, 2 * NB)
                for half in range(2):
                    sp.dma_start(wout_in[M * half:M * (half + 1), :], Wout).then_inc(wout_loaded, 16)

            def next_k_diag(b):
                sp.wait_ge(maxs_done[1], b * SQ // TOK * MAX_TILES)
                for gr in range(G):
                    sp.dma_start(k_diag[HD * gr:HD * (gr + 1), :, gr * KV:(gr + 1) * KV].bitcast(F32),
                                 k_stack[b][0:HD, HC * gr:HC * (gr + 1), :].bitcast(F32)).then_inc(k_diag_done, 16)

            def load_x(T, j):
                sp.wait_ge(z1_turned, T * TB + j + 1 - TB)
                sp.dma_start(xin[:, j, :], x_t[T, j]).then_inc(x_loaded[j], 16)

            def load_residual(T, j):
                if first(T):
                    if j == 0:
                        sp.wait_ge(weights_split, WEIGHTS)
                else:
                    sp.wait_ge(stored[j], T * 16)
                sp.dma_start(x1[:, j, :], x_t[T, j]).then_inc(xr_loaded[j], 16)

            def stack_q(T, gr):
                if gr == 0:
                    sp.wait_ge(qt_lo_done, T * TB + TB)
                if not first(T):
                    sp.wait_ge(scores_done, T * H + (gr + 1) * HC - H)
                rows, heads = slice(HD * gr, HD * (gr + 1)), slice(HC * gr, HC * (gr + 1))
                for part, src in enumerate((qt_hi, qt_lo, qt_hi)):
                    sp.dma_start(q_stack[HD * part:HD * (part + 1), heads, :].bitcast(F32),
                                 src[rows, :, :].bitcast(F32)).then_inc(stacked[gr], 16)

            def stack_max(T, half):
                sp.wait_ge(mxt_done, T + 1)
                if not first(T):
                    sp.wait_ge(scores_done, T * H + H // 2 * (half + 1) - H)
                sp.dma_start(q_stack[3 * HD:3 * HD + 1, H // 2 * half:H // 2 * (half + 1), :].bitcast(F32),
                             mxt[H // 2 * half:H // 2 * (half + 1), :].bitcast(F32)).then_inc(max_stacked[half], 16)

            def store(T, j):
                sp.wait_ge(out_done, T * TB + j + 1)
                sp.dma_start(out_t[T, j], x1[:, j, :]).then_inc(stored[j], 16)

            def iteration(t, kb, kf, g, f, a, b):
                N, F, B, prologue = t + 2, t + 1, t - 1, isinstance(t, int) and t == -1
                if g:
                    load_x(N, 0)
                if b:
                    load_residual(B, 0)
                    load_residual(B, 1)
                if g:
                    load_x(N, 1)
                    load_x(N, 2)
                    load_x(N, 3)
                if prologue:
                    stack_keys(0)
                    load_wout()
                if b:
                    load_residual(B, 2)
                if a:
                    stack_max(t, 0)
                if b:
                    load_residual(B, 3)
                if a:
                    stack_max(t, 1)
                if isinstance(t, int) and t == 0:
                    stack_keys(1)
                if kb != kf:
                    next_k_diag(kf)
                if b:
                    store(B, 0)
                if f:
                    stack_q(F, 0)
                    stack_q(F, 1)
                    stack_q(F, 2)
                    stack_q(F, 3)
                if b:
                    store(B, 1)
                    store(B, 2)
                    store(B, 3)

            iteration(-1, 0, 0, True, True, False, False)
            iteration(0, 0, 0, True, True, True, False)
            iteration(1, 0, 0, True, True, True, True)
            with sp.Fori(2, BLOCKS // NB - 1) as t:
                iteration(t, 0, 0, True, True, True, True)
            iteration(BLOCKS // NB - 1, 0, 1, True, True, True, True)
            with sp.Fori(BLOCKS // NB, BLOCKS - 2) as t:
                iteration(t, 1, 1, True, True, True, True)
            iteration(BLOCKS - 2, 1, 1, False, True, True, True)
            iteration(BLOCKS - 1, 1, 1, False, False, True, True)
            iteration(BLOCKS, 1, 1, False, False, False, True)
            for j in range(TB):
                sp.wait_ge(stored[j], BLOCKS * 16)

        @block.gpsimd
        def _(pool):
            pool.memset(ident[:, :], 0.0).then_inc(eyes, 1)
            pool.memset(b2_col[:, :], 0.0).then_inc(eyes, 1)
            pool.memset(bc_sel_f[:, :, :], 0.0).then_inc(eyes, 1)
            pool.memset(den_sel[:, :, :], 0.0).then_inc(eyes, 1)
            pool.wait_ge(eyes, NEYES)
            pool.affine_select(out=ident[:, :], in_=ident[:, :], compare_op=ALU.not_equal, fill=1.0,
                               base=0, pattern=[[-1, P]], channel_multiplier=1).then_inc(consts, 1)
            sel = bc_sel_f[:, :, :].rearrange("p c (a i d) -> p c a i d", a=2, i=2)
            for a in range(2):
                pool.affine_select(out=sel[:, :, a], in_=sel[:, :, a], compare_op=ALU.not_equal, fill=1.0,
                                   base=-2 * HD * (1 - a), pattern=[[-8, C], [-HD, 2], [0, HD]],
                                   channel_multiplier=1).then_inc(consts, 1)
            for c in range(C):
                pool.memset(den_sel[:, c, 8 * c:8 * c + 8], 1.0).then_inc(consts, 1)
            pool.memset(k_diag[:, :, :].bitcast(F32), 0.0).then_inc(k_diag_done, 1)
            pool.wait_ge(k_diag_done, 1)
            for b in range(NB):
                pool.wait_ge(consts, 3 + C + b)
                pool.memset(k_stack[b][3 * HD:3 * HD + 1, :, :].bitcast(F32), -1.0).then_inc(consts, 1)

            def split_weights():
                pool.wait_ge(wo_hi_done, 4)
                pool.tensor_tensor(wo_lo[:, :, :], wo_in[:, :, :], wo_hi[:, :, :].bitcast(F32),
                                   ALU.subtract).then_inc(weights_split, 1)
                for half in range(2):
                    pool.tensor_tensor(win_lo[:, :, half, :], win_in, win_hi[:, :, half, :].bitcast(F32),
                                       ALU.subtract).then_inc(weights_split, 1)
                pool.wait_ge(params_loaded, PARAMS)
                pool.tensor_tensor(wout_lo[:, :], wout_in, wout_hi[:, :].bitcast(F32),
                                   ALU.subtract).then_inc(weights_split, 1)
                for hh in range(HH):
                    pool.tensor_scalar(w2_diag[:, hh, :], pair_eye, w2_col[:, hh:hh + 1], 0.0, ALU.mult,
                                       ALU.add).then_inc(weights_split, 1)

            def square(T, j):
                pool.wait_ge(u_done, T * TB + j + 1)
                if not (first(T) and j == 0):
                    pool.wait_ge(ssq_done, T * TB + j)
                if j == 0 and not (isinstance(T, int) and T <= 1):
                    pool.wait_ge(rden_lo_done, T - 1)
                pool.tensor_tensor(sq, u[:, j, :], u[:, j, :], ALU.mult).then_inc(sq_done, 1)

            def q_low(T, j):
                cols = slice(j * P, (j + 1) * P)
                pool.wait_ge(qf_done, T * TB + j + 1)
                pool.tensor_tensor(qt_lo[:, :, cols], u[:, j, :].rearrange("p (i n) -> p i n", i=HC),
                                   qt_hi[:, :, cols].bitcast(F32), ALU.subtract).then_inc(qt_lo_done, 1)

            def att_low(T, c):
                pool.wait_ge(at_hi_done, T * C + c + 1)
                pool.tensor_tensor(at_lo[:, c, :], att[:, c, :], at_hi[:, c, :].bitcast(F32),
                                   ALU.subtract).then_inc(at_lo_done, 1)

            def add_bout(T, j):
                pool.wait_ge(z2_done, T * TB + j + 1)
                pool.tensor_tensor(x1[:, j, :], x1[:, j, :], bout_row[:, :], ALU.add).then_inc(bout_added, 1)

            def iteration(t, kb, kf, g, f, a, b):
                F, B, prologue = t + 1, t - 1, isinstance(t, int) and t == -1
                if f:
                    square(F, 0)
                if b:
                    att_low(B, 0)
                    att_low(B, 1)
                    att_low(B, 2)
                    att_low(B, 3)
                if f:
                    square(F, 1)
                    square(F, 2)
                    square(F, 3)
                if b:
                    add_bout(B, 0)
                if f:
                    q_low(F, 0)
                if b:
                    add_bout(B, 1)
                if f:
                    q_low(F, 1)
                if b:
                    add_bout(B, 2)
                if f:
                    q_low(F, 2)
                if b:
                    add_bout(B, 3)
                if f:
                    q_low(F, 3)
                if prologue:
                    split_weights()

            def last(B):
                att_low(B, 0)
                att_low(B, 2)
                for j in range(TB):
                    add_bout(B, j)

            iterations(pool, iteration, last)

        @block.vector
        def _(dve):
            heads = lambda a, n: a.rearrange("p (h d) -> p h d", h=n)

            def newton(buf, v, n_in, act_sem, act_value, step_sem, base):
                y, a, c2 = buf[:, 1, :], buf[:, 2, :], buf[:, 3, :]
                dve.wait_ge(act_sem, act_value)
                dve.tensor_tensor(a, y, y, ALU.mult).then_inc(step_sem, 1)
                dve.wait_ge(step_sem, base + 1)
                dve.scalar_tensor_tensor(out=a, in0=v, scalar=EPS * n_in, in1=a, op0=ALU.add,
                                         op1=ALU.mult).then_inc(step_sem, 1)
                dve.wait_ge(step_sem, base + 2)
                dve.tensor_scalar(a, a, -0.5 / n_in, 1.5, ALU.mult, ALU.add).then_inc(step_sem, 1)
                dve.wait_ge(step_sem, base + 3)
                dve.tensor_tensor(c2, y, a, ALU.mult).then_inc(step_sem, 1)
                dve.wait_ge(step_sem, base + 4)

            def split_wq(c):
                wqh = wq_in[:, c, :].rearrange("p (h d) -> p h d", h=H)
                mean = lnq[:, 0, c * H:(c + 1) * H]
                dve.wait_ge(wq_loaded[c], 16)
                dve.tensor_reduce(mean, wqh, AX.X, ALU.add).then_inc(wq_step, 1)
                dve.wait_ge(wq_step, 3 * c + 1)
                dve.tensor_scalar(mean, mean, 1.0 / HD, None, ALU.mult).then_inc(wq_step, 1)
                dve.wait_ge(wq_step, 3 * c + 2)
                dve.tensor_tensor(wqh, wqh, mean.unsqueeze(2).broadcast_to([P, H, HD]),
                                  ALU.subtract).then_inc(wq_step, 1)

            def wq_low(c):
                dve.wait_ge(wq_hi_done, c + 1)
                dve.tensor_tensor(wq_lo[:, c, :].rearrange("p (i g d) -> p i g d", i=HC, g=G),
                                  by_place(wq_in[:, c, :]),
                                  wq_hi[:, c, :].rearrange("p (i g d) -> p i g d", i=HC, g=G).bitcast(F32),
                                  ALU.subtract).then_inc(wq_split, 1)

            kh = keys.rearrange("p b (h d) -> p (b h) d", h=H)
            kh2 = keys2.rearrange("p b (h d) -> p (b h) d", h=H)
            per_head = lambda a: a.unsqueeze(2).broadcast_to([P, NB * H, HD])
            on_heads = lambda a: a.unsqueeze(1).broadcast_to([P, NB * H, HD])

            def key_norm(part):
                if part == 0:
                    dve.wait_ge(keys_moved, NB)
                    dve.tensor_reduce(kst[:, 4, :], kh, AX.X, ALU.add).then_inc(key_step, 1)
                    dve.wait_ge(key_step, 1)
                    dve.tensor_scalar(kst[:, 4, :], kst[:, 4, :], 1.0 / HD, None, ALU.mult).then_inc(key_step, 1)
                    dve.wait_ge(key_step, 2)
                    dve.tensor_tensor(kh, kh, per_head(kst[:, 4, :]), ALU.subtract).then_inc(key_step, 1)
                elif part == 1:
                    dve.wait_ge(key_step, 3)
                    dve.tensor_tensor(kh2, kh, kh, ALU.mult).then_inc(key_step, 1)
                    dve.wait_ge(key_step, 4)
                    dve.tensor_reduce(kst[:, 5, :], kh2, AX.X, ALU.add).then_inc(key_step, 1)
                elif part == 2:
                    newton(kst, kst[:, 5, :], HD, key_guess, 2, key_step, 5)
                    dve.tensor_tensor(kh, kh, per_head(kst[:, 3, :]), ALU.mult).then_inc(key_step, 1)
                else:
                    dve.wait_ge(key_step, 10)
                    dve.wait_ge(params_loaded, PARAMS)
                    dve.tensor_tensor(kh, kh, on_heads(gk_row[:, :]), ALU.mult).then_inc(key_step, 1)
                    dve.wait_ge(key_step, 11)
                    for b in range(NB):
                        dve.tensor_tensor(keys2[:, b, :].rearrange("p (i g d) -> p i g d", i=HC, g=G),
                                          by_place(keys[:, b, :]),
                                          bk_row[:, :].unsqueeze(1).unsqueeze(1).broadcast_to([P, HC, G, HD]),
                                          ALU.add).then_inc(key_step, 1)

            def keys_low():
                for b in range(NB):
                    dve.wait_ge(keys_hi_done, b + 1)
                    dve.tensor_tensor(kn_lo[:, b, :], (AT, DEN)[b][:, :], kn_hi[:, b, :].bitcast(F32),
                                      ALU.subtract).then_inc(keys_split, 1)

            def aggregate(bn, mv, bn_sem, mv_sem, count):
                dve.wait_ge(bn_sem, count)
                dve.tensor_copy(spare[:, :], bn[:, 0, 0:1])
                for j in range(TB):
                    dve.bn_aggr(mv[:, j, :], bn[:, j, :]).then_inc(mv_sem, 1)

            def stats1(T, j):
                dve.wait_ge(x_loaded[j], T * 16 + 16)
                dve.bn_stats(bn1[:, j, :], xin[:, j, :]).then_inc(bn1_done, 1)

            def aggregate1(T):
                aggregate(bn1, mv1, bn1_done, mv1_done, T * TB + TB)

            def newton1(T):
                newton(ln1, mv1[:, :, 1], 1, ln1_act, T * 2 + 2, ln1_step, T * 4)

            def z1_norm(T, j):
                dve.tensor_scalar(xin[:, j, :], xin[:, j, :], mv1[:, j, 0:1], ln1[:, 3, j:j + 1],
                                  ALU.subtract, ALU.mult).then_inc(z1_done, 1)

            def z1_low(T, j):
                dve.wait_ge(zt_hi_done, T * TB + j + 1)
                dve.tensor_tensor(zt_lo[:, j % 2, :, :].rearrange("p c n -> p (c n)"), z1_bank[j][:, :],
                                  zt_hi[:, j % 2, :, :].rearrange("p c n -> p (c n)").bitcast(F32),
                                  ALU.subtract).then_inc(zt_lo_done, 1)

            def sum_squares(T, j):
                dve.wait_ge(sq_done, T * TB + j + 1)
                dve.tensor_reduce(ssq[:, j, :], heads(sq, H), AX.X, ALU.add).then_inc(ssq_done, 1)

            def newton_q(T):
                newton(lnq, ssq[:, :, :].rearrange("p j h -> p (j h)"), HD, lnq_act, T * 2 + 2, lnq_step, T * 4)

            def norm_q(T, j):
                uj = heads(u[:, j, :], H)
                dve.tensor_tensor(uj, uj, lnq[:, 3, j * H:(j + 1) * H].unsqueeze(2).broadcast_to([P, H, HD]),
                                  ALU.mult).then_inc(un_done, 1)

            def q_full(T, j):
                dve.wait_ge(qt_hi_done, T * TB + j + 1)
                dve.tensor_scalar(u[:, j, :], qt_bank[j][:, :], gq_col[:, 0:1], bq_col[:, 0:1], ALU.mult,
                                  ALU.add).then_inc(qf_done, 1)

            def row_max(T, i, j):
                half, tile = i // 2, i % 2 * TB + j
                dve.wait_ge(maxs_done[half], T * MAX_TILES + tile + 1)
                if half == 0 and tile == 0 and not first(T):
                    dve.wait_ge(mx_turned, T)
                dve.tensor_reduce(mx[:, j, :].rearrange("p (g i) -> p i g", g=G)[:, i, :],
                                  maxs_bank[i][j][:, :].rearrange("p (g n) -> p g n", g=G), AX.X,
                                  ALU.max).then_inc(mx_done[half], 1)

            def reciprocal(t):
                dve.wait_ge(pv_done, t * PAIRS + PAIRS)
                dve.reciprocal(rden[:, :], DEN[:, :]).then_inc(rden_done, 1)

            def rden_low(t):
                dve.wait_ge(rden_hi_done, t + 1)
                dve.tensor_tensor(rden_lo, rden[:, :], rden_hi.bitcast(F32),
                                  ALU.subtract).then_inc(rden_lo_done, 1)

            def normalise(T, c):
                dve.wait_ge(spread_done, T * C + c + 1)
                dve.wait_ge(att_moved, T * C + c + 1)
                dve.tensor_tensor(att[:, c, :], spread_bank[c][:, :], att[:, c, :], ALU.mult).then_inc(att_done, 1)

            def residual1(T, j):
                dve.wait_ge(o_done, T * TB + j + 1)
                dve.wait_ge(xr_loaded[j], T * 16 + 16)
                dve.tensor_tensor(x1[:, j, :], o_bank[j][:, :], x1[:, j, :], ALU.add).then_inc(x1_done, 1)

            def stats2(T, j):
                dve.wait_ge(x1_done, T * TB + j + 1)
                dve.bn_stats(bn2[:, j, :], x1[:, j, :]).then_inc(bn2_done, 1)

            def aggregate2(T):
                aggregate(bn2, mv2, bn2_done, mv2_done, T * TB + TB)

            def newton2(T):
                newton(ln2, mv2[:, :, 1], 1, ln2_act, T * 2 + 2, ln2_step, T * 4)

            def z2_norm(T, j):
                if j >= 2:
                    dve.wait_ge(z2_turned, T * TB + j - 1)
                dve.tensor_scalar(z2[:, j % 2, :], x1[:, j, :], mv2[:, j, 0:1], ln2[:, 3, j:j + 1],
                                  ALU.subtract, ALU.mult).then_inc(z2_done, 1)

            def z2_low(T, j):
                cols = slice(j * P, (j + 1) * P)
                dve.wait_ge(z2t_hi_done, T * TB + j + 1)
                dve.tensor_tensor(z2t_lo[:, :, cols], z2_bank[j][:, :].rearrange("p (c n) -> p c n", c=C),
                                  z2t_hi[:, :, cols].bitcast(F32), ALU.subtract).then_inc(z2t_lo_done, 1)

            def g_low(T):
                dve.wait_ge(g_hi_done, T + 1)
                dve.scalar_tensor_tensor(out=g_lo, in0=g_bank[:, :], scalar=b2_col[:, 0:1], in1=g_hi.bitcast(F32),
                                         op0=ALU.add, op1=ALU.subtract).then_inc(g_done, 1)

            def residual2(T, j):
                dve.wait_ge(y_done, T * TB + j + 1)
                dve.wait_ge(bout_added, T * TB + j + 1)
                dve.tensor_tensor(x1[:, j, :], y_bank[j][:, :], x1[:, j, :], ALU.add).then_inc(out_done, 1)

            for j in range(TB):
                stats1(0, j)
            aggregate1(0)
            split_wq(0)
            newton1(0)
            for j in range(TB):
                z1_norm(0, j)
            split_wq(1)
            split_wq(2)
            wq_low(0)
            split_wq(3)
            for c in range(1, C):
                wq_low(c)
            dve.wait_ge(consts, NCONSTS)
            dve.tensor_copy(bc_sel[:, :, :], bc_sel_f[:, :, :]).then_inc(wq_split, 1)
            dve.tensor_tensor(pair_eye, ident[:, 0:M], ident[:, M:2 * M], ALU.add).then_inc(wq_split, 1)

            def iteration(t, kb, kf, g, f, a, b):
                N, F, B, prologue = t + 2, t + 1, t - 1, isinstance(t, int) and t == -1
                if f:
                    z1_low(F, 0)
                    z1_low(F, 1)
                if prologue:
                    key_norm(0)
                    key_norm(1)
                if b:
                    normalise(B, 0)
                    normalise(B, 1)
                if a:
                    row_max(t, 2, 0)
                if b:
                    normalise(B, 2)
                    normalise(B, 3)
                if f:
                    z1_low(F, 2)
                if a:
                    row_max(t, 2, 1)
                if f:
                    sum_squares(F, 0)
                if a:
                    row_max(t, 2, 2)
                if f:
                    z1_low(F, 3)
                if prologue:
                    key_norm(2)
                    key_norm(3)
                if a:
                    row_max(t, 2, 3)
                    row_max(t, 3, 0)
                if g:
                    stats1(N, 0)
                if a:
                    row_max(t, 3, 1)
                    row_max(t, 3, 2)
                    row_max(t, 3, 3)
                if g:
                    stats1(N, 1)
                if f:
                    sum_squares(F, 1)
                if g:
                    stats1(N, 2)
                if b:
                    residual1(B, 0)
                    stats2(B, 0)
                if g:
                    stats1(N, 3)
                    aggregate1(N)
                if f:
                    sum_squares(F, 2)
                if g:
                    newton1(N)
                    z1_norm(N, 0)
                if f:
                    sum_squares(F, 3)
                if prologue:
                    keys_low()
                if b:
                    residual1(B, 1)
                    stats2(B, 1)
                if g:
                    z1_norm(N, 1)
                if b:
                    residual1(B, 2)
                if g:
                    z1_norm(N, 2)
                if b:
                    stats2(B, 2)
                if f:
                    newton_q(F)
                if b:
                    residual1(B, 3)
                    stats2(B, 3)
                    aggregate2(B)
                if f:
                    norm_q(F, 0)
                    norm_q(F, 1)
                if b:
                    newton2(B)
                if f:
                    norm_q(F, 2)
                if b:
                    z2_norm(B, 0)
                if g:
                    z1_norm(N, 3)
                if b:
                    z2_norm(B, 1)
                if f:
                    norm_q(F, 3)
                    q_full(F, 0)
                if b:
                    z2_norm(B, 2)
                    z2_norm(B, 3)
                    z2_low(B, 0)
                    z2_low(B, 1)
                    z2_low(B, 2)
                    z2_low(B, 3)
                if f:
                    q_full(F, 1)
                    row_max(F, 0, 0)
                    q_full(F, 2)
                    row_max(F, 0, 1)
                    row_max(F, 0, 2)
                if a:
                    reciprocal(t)
                if f:
                    q_full(F, 3)
                if b:
                    g_low(B)
                if f:
                    row_max(F, 0, 3)
                if a:
                    rden_low(t)
                if b:
                    residual2(B, 0)
                    residual2(B, 1)
                if f:
                    row_max(F, 1, 0)
                if b:
                    residual2(B, 2)
                    residual2(B, 3)
                if f:
                    row_max(F, 1, 1)
                    row_max(F, 1, 2)
                    row_max(F, 1, 3)

            def att_low(T, c):
                dve.wait_ge(at_hi_done, T * C + c + 1)
                dve.tensor_tensor(at_lo[:, c, :], att[:, c, :], at_hi[:, c, :].bitcast(F32),
                                  ALU.subtract).then_inc(at_lo_done, 1)

            def norm2_half(T, half):
                tiles = slice(2 * half, 2 * half + 2)
                dve.wait_ge(bn2_done, T * TB + 2 * half + 2)
                dve.tensor_copy(spare[:, :], bn2[:, 0, 0:1])
                for j in (2 * half, 2 * half + 1):
                    dve.bn_aggr(mv2[:, j, :], bn2[:, j, :]).then_inc(mv2_done, 1)
                newton(ln2[:, :, tiles], mv2[:, tiles, 1], 1, ln2_act, T * 2 + 2 + 2 * half, ln2_step, T * 4 + 4 * half)
                z2_norm(T, 2 * half)
                z2_norm(T, 2 * half + 1)

            def hidden(T, hh):
                dve.wait_ge(s_done, T + 1)
                if hh >= RR:
                    dve.wait_ge(hsum_done, T * HH + hh + 1 - RR)
                dve.tensor_scalar(hid[:, hh % RR, :], s_in[:, :], w1_col[:, hh:hh + 1], b1_col[:, hh:hh + 1], ALU.mult,
                                  ALU.add).then_inc(odd_step, 1)
                dve.wait_ge(odd_step, hh // 2 + 1)
                dve.tensor_scalar(hid[:, hh % RR, :], hid[:, hh % RR, :], 0.0, None, ALU.max).then_inc(odd_hidden, 1)

            def last(B):
                normalise(B, 0)
                normalise(B, 1)
                normalise(B, 2)
                att_low(B, 1)
                normalise(B, 3)
                att_low(B, 3)
                residual1(B, 0)
                stats2(B, 0)
                residual1(B, 1)
                stats2(B, 1)
                norm2_half(B, 0)
                residual1(B, 2)
                stats2(B, 2)
                z2_low(B, 0)
                z2_low(B, 1)
                residual1(B, 3)
                stats2(B, 3)
                norm2_half(B, 1)
                z2_low(B, 2)
                z2_low(B, 3)
                for hh in range(1, HH, 2):
                    hidden(B, hh)
                g_low(B)
                for j in range(TB):
                    residual2(B, j)

            iterations(dve, iteration, last)

        @block.scalar
        def _(act):
            def rsqrt_guess(v, buf, n_in, in_sem, in_value, act_sem, act_value):
                act.wait_ge(in_sem, in_value)
                act.activation(buf[:, 0, :], v, ACT.Ln, bias=EPS, scale=1.0 / n_in).then_inc(act_sem, 1)
                act.wait_ge(act_sem, act_value - 1)
                act.activation(buf[:, 1, :], buf[:, 0, :], ACT.Exp, scale=-0.5).then_inc(act_sem, 1)

            def guess1(T):
                rsqrt_guess(mv1[:, :, 1], ln1, 1, mv1_done, T * TB + TB, ln1_act, T * 2 + 2)

            def guess2(T):
                rsqrt_guess(mv2[:, :, 1], ln2, 1, mv2_done, T * TB + TB, ln2_act, T * 2 + 2)

            def guess_q(T):
                rsqrt_guess(ssq[:, :, :].rearrange("p j h -> p (j h)"), lnq, HD, ssq_done, T * TB + TB,
                            lnq_act, T * 2 + 2)

            def z1_high(T, j):
                act.wait_ge(z1_turned, T * TB + j + 1)
                if j >= 2:
                    act.wait_ge(q_done, T * TB + j - 1)
                act.activation(zt_hi[:, j % 2, :, :].rearrange("p c n -> p (c n)"), z1_bank[j][:, :],
                               ACT.Copy).then_inc(zt_hi_done, 1)

            def move_u(T, j):
                act.wait_ge(q_done, T * TB + j + 1)
                if not first(T):
                    act.wait_ge(qt_lo_done, T * TB + j + 1 - TB)
                act.activation(u[:, j, :], q_bank[j][:, :], ACT.Copy).then_inc(u_done, 1)

            def q_high(T, j):
                act.wait_ge(q_turned, T * TB + j + 1)
                if j == 0 and not first(T):
                    for gr in range(G):
                        act.wait_ge(stacked[gr], T * 48)
                    act.wait_ge(maxs_done[1], T * MAX_TILES)
                act.activation(qt_hi[:, :, j * P:(j + 1) * P], qt_bank[j][:, :].rearrange("p (i n) -> p i n", i=HC),
                               ACT.Identity, bias=bq_col[:, 0:1], scale=gq_col[:, 0:1]).then_inc(qt_hi_done, 1)

            def move_max(T):
                act.wait_ge(mx_turned, T + 1)
                if not first(T):
                    for half in range(2):
                        act.wait_ge(max_stacked[half], T * 16)
                act.activation(mxt[:, :], mxt_bank[0:H, :], ACT.Copy).then_inc(mxt_done, 1)

            def exponential(t, h):
                act.wait_ge(scores_done, t * H + h + 1)
                if h >= PR or not first(t):
                    act.wait_ge(pv_done, t * PAIRS + (h - PR) // 2 + 1)
                act.activation(prob[:, h % PR, :], score_bank[h][:, :], ACT.Exp, scale=SCALE).then_inc(exp_done, 1)

            def move_att(t, c):
                act.wait_ge(pv_done, t * PAIRS + 2 * (c + 1))
                if not first(t):
                    act.wait_ge(at_lo_done, t * C + c + 1 - C)
                act.activation(att[:, c, :], AT[:, :], ACT.Copy).then_inc(att_moved, 1)

            def rden_high(t):
                act.wait_ge(rden_done, t + 1)
                if not first(t):
                    act.wait_ge(s_mm_done, t)
                act.activation(rden_hi, rden[:, :], ACT.Copy).then_inc(rden_hi_done, 1)

            def att_high(T, c):
                act.wait_ge(att_done, T * C + c + 1)
                act.activation(at_hi[:, c, :], att[:, c, :], ACT.Copy).then_inc(at_hi_done, 1)

            def z2_high(T, j):
                act.wait_ge(z2_turned, T * TB + j + 1)
                act.wait_ge(o_done, T * TB + j + 1)
                act.activation(z2t_hi[:, :, j * P:(j + 1) * P], z2_bank[j][:, :].rearrange("p (c n) -> p c n", c=C),
                               ACT.Copy).then_inc(z2t_hi_done, 1)

            def move_s(T):
                act.wait_ge(s_mm_done, T + 1)
                act.activation(s_in[:, :], s_bank[:, :], ACT.Identity, bias=bin_col[:, 0:1]).then_inc(s_done, 1)

            def hidden(T, hh):
                act.wait_ge(s_done, T + 1)
                if hh >= RR:
                    act.wait_ge(hsum_done, T * HH + hh + 1 - RR)
                act.activation(hid[:, hh % RR, :], s_in[:, :], ACT.Relu, bias=b1_col[:, hh:hh + 1],
                               scale=w1_col[:, hh:hh + 1]).then_inc(hid_done, 1)

            def g_high(T):
                act.wait_ge(hsum_done, T * HH + HH)
                act.activation(g_hi, g_bank[:, :], ACT.Identity, bias=b2_col[:, 0:1]).then_inc(g_hi_done, 1)

            act.preload_act_table_set("natural_log_exp_and_others")
            guess1(0)
            for c in range(C):
                if c == 1:
                    for b in range(NB):
                        act.wait_ge(ctx_turned, b + 1)
                        act.activation(ctx_t[:, b, :], (AT, DEN)[b][:, :], ACT.Copy).then_inc(ctx_moved, 1)
                act.wait_ge(wq_step, 3 * c + 3)
                act.activation(wq_hi[:, c, :].rearrange("p (i g d) -> p i g d", i=HC, g=G), by_place(wq_in[:, c, :]),
                               ACT.Copy).then_inc(wq_hi_done, 1)

            def move_keys(b):
                act.wait_ge(kv_projected, b + 1)
                act.activation(keys[:, b, :], (AT, DEN)[b][:, :], ACT.Copy).then_inc(keys_moved, 1)

            def move_values():
                for b in range(NB):
                    act.wait_ge(kv_projected, NB + b + 1)
                    act.activation(v_kv[b][:, :], value_bank[b][:, :], ACT.Copy).then_inc(values_moved, 1)

            def turned_keys():
                for b in range(NB):
                    act.wait_ge(keys_turned, b + 1)
                    act.activation(kn_hi[:, b, :], (AT, DEN)[b][:, :], ACT.Copy).then_inc(keys_hi_done, 1)
                act.wait_ge(k_diag_done, 1)
                act.wait_ge(keys_hi_done, 1)
                for gr in range(G):
                    rows = slice(HD * gr, HD * (gr + 1))
                    act.activation(k_diag[rows, :, gr * KV:(gr + 1) * KV],
                                   kn_hi[rows, 0, :].rearrange("p (i n) -> p i n", i=HC).bitcast(F32),
                                   ACT.Copy).then_inc(k_diag_done, 1)

            def split_weights():
                act.wait_ge(wo_loaded, 32)
                act.activation(wo_hi[:, :, :], wo_in[:, :, :], ACT.Copy).then_inc(wo_hi_done, 1)
                for half in range(2):
                    act.activation(win_hi[:, :, half, :], win_in, ACT.Copy).then_inc(wo_hi_done, 1)
                act.wait_ge(wout_loaded, 32)
                act.activation(wout_hi[:, :], wout_in, ACT.Copy).then_inc(wo_hi_done, 1)

            def iteration(t, kb, kf, g, f, a, b):
                N, F, B, prologue = t + 2, t + 1, t - 1, isinstance(t, int) and t == -1
                if f:
                    z1_high(F, 0)
                    z1_high(F, 1)
                if prologue:
                    move_keys(0)
                    move_keys(1)
                if b:
                    att_high(B, 0)
                    att_high(B, 1)
                if f:
                    move_u(F, 0)
                    z1_high(F, 2)
                if b:
                    att_high(B, 2)
                if f:
                    z1_high(F, 3)
                if prologue:
                    rsqrt_guess(kst[:, 5, :], kst, HD, key_step, 5, key_guess, 2)
                if b:
                    att_high(B, 3)
                if f:
                    move_u(F, 1)
                    move_u(F, 2)
                if a:
                    move_max(t)
                if f:
                    move_u(F, 3)
                if prologue:
                    turned_keys()
                if g:
                    guess1(N)
                if a:
                    exponential(t, 0)
                    exponential(t, 1)
                    exponential(t, 2)
                if f:
                    guess_q(F)
                if prologue:
                    move_values()
                    act.wait_ge(params_loaded, PARAMS)
                if a:
                    exponential(t, 3)
                    exponential(t, 4)
                    exponential(t, 5)
                if b:
                    guess2(B)
                if a:
                    move_att(t, 0)
                    exponential(t, 6)
                    exponential(t, 7)
                if f:
                    q_high(F, 0)
                if a:
                    exponential(t, 8)
                    exponential(t, 9)
                    move_att(t, 1)
                    exponential(t, 10)
                if b:
                    z2_high(B, 0)
                    z2_high(B, 1)
                if a:
                    exponential(t, 11)
                if f:
                    q_high(F, 1)
                if b:
                    z2_high(B, 2)
                    z2_high(B, 3)
                if a:
                    exponential(t, 12)
                    exponential(t, 13)
                    move_att(t, 2)
                if f:
                    q_high(F, 2)
                if a:
                    exponential(t, 14)
                    exponential(t, 15)
                if b:
                    move_s(B)
                    hidden(B, 0)
                    hidden(B, 1)
                    hidden(B, 2)
                    hidden(B, 3)
                    hidden(B, 4)
                    hidden(B, 5)
                    hidden(B, 6)
                    hidden(B, 7)
                if f:
                    q_high(F, 3)
                if prologue:
                    split_weights()
                if b:
                    g_high(B)
                if a:
                    rden_high(t)
                    move_att(t, 3)

            def enter():
                act.wait_ge(keys_stacked, 16 * NB * G * 3)

            def last(B):
                for c in range(C):
                    att_high(B, c)
                for half in range(2):
                    tiles = slice(2 * half, 2 * half + 2)
                    rsqrt_guess(mv2[:, tiles, 1], ln2[:, :, tiles], 1, mv2_done, B * TB + 2 * half + 2, ln2_act,
                                B * 2 + 2 + 2 * half)
                    z2_high(B, 2 * half)
                    z2_high(B, 2 * half + 1)
                move_s(B)
                for hh in range(0, HH, 2):
                    hidden(B, hh)
                g_high(B)

            iterations(act, iteration, last, enter)

        @block.tensor
        def _(pe):
            def last_user(*users):
                for there, semaphore, value in users:
                    if there:
                        pe.wait_ge(semaphore, value)
                        return

            def three_pass(dst, pairs):
                terms = [t for (lh, ll, rh, rl) in pairs for t in ((lh, rh), (lh, rl), (ll, rh))]
                for n, (l, r) in enumerate(terms):
                    ins = pe.matmul(dst, l, r, start=n == 0, stop=n == len(terms) - 1)
                return ins

            def turn(dst, src, done):
                for n in range(4):
                    ins = pe.transpose(dst[:, n * P:(n + 1) * P], src(n), ident[:, :])
                ins.then_inc(done, 1)

            columns = lambda a: lambda n: a[:, n * P:(n + 1) * P]

            pe.wait_ge(consts, 1)
            pe.wait_ge(ctx_loaded, 16)
            for b in range(NB):
                turn((AT, DEN)[b], columns(ctx_in[:, b, :]), ctx_turned)
            def project_kv(dst, b, w):
                for c in range(C):
                    ins = pe.matmul(dst[:, :], ctx_t[:, b, c * P:(c + 1) * P], w[:, c, :], start=c == 0,
                                    stop=c == C - 1)
                ins.then_inc(kv_projected, 1)

            def project_keys():
                pe.wait_ge(ctx_moved, NB)
                pe.wait_ge(wk_loaded, 16)
                for b in range(NB):
                    project_kv((AT, DEN)[b], b, wk_in)

            def project_values():
                pe.wait_ge(wv_loaded, 16)
                pe.wait_ge(u_done, TB - 1)
                for b in range(NB):
                    project_kv(value_bank[b], b, wv_in)
                pe.wait_ge(consts, NCONSTS)
                pe.wait_ge(values_moved, NB)

            def turn_z1(T, j):
                pe.wait_ge(z1_done, T * TB + j + 1)
                turn(z1_bank[j], columns(xin[:, j, :]), z1_turned)

            def project_q(T, j):
                pe.wait_ge(zt_lo_done, T * TB + j + 1)
                three_pass(q_bank[j][:, :], [(zt_hi[:, j % 2, c, :], zt_lo[:, j % 2, c, :], wq_hi[:, c, :], wq_lo[:, c, :])
                                             for c in range(C)]).then_inc(q_done, 1)

            def turn_keys():
                pe.wait_ge(key_step, 13)
                for b in range(NB):
                    turn((AT, DEN)[b], columns(keys2[:, b, :]), keys_turned)
    
            def turn_q(T, j):
                pe.wait_ge(un_done, T * TB + j + 1)
                turn(qt_bank[j], columns(u[:, j, :]), q_turned)

            def max_scores(T, kb, i, j):
                if i == 0:
                    pe.wait_ge(qt_hi_done, T * TB + j + 1)
                    if j == 0:
                        pe.wait_ge(k_diag_done, 1 + G + kb * 16 * G)
                pe.matmul(maxs_bank[i][j][:, :], qt_hi[:, i, j * P:(j + 1) * P], k_diag[:, i, :], start=True,
                          stop=True).then_inc(maxs_done[i // 2], 1)

            def turn_max(T):
                for half in range(2):
                    pe.wait_ge(mx_done[half], (T + 1) * MAX_TILES)
                for j in range(TB):
                    ins = pe.transpose(mxt_bank[0:H, j * P:(j + 1) * P], mx[:, j, :], ident[:, :])
                ins.then_inc(mx_turned, 1)

            def scores(t, kb, h):
                if h % HC == 0:
                    pe.wait_ge(stacked[h // HC], t * 48 + 48)
                if h % (H // 2) == 0:
                    pe.wait_ge(max_stacked[h // (H // 2)], t * 16 + 16)
                pe.matmul(score_bank[h][:, :], k_stack[kb][0:3 * HD + 1, h, :], q_stack[0:3 * HD + 1, h, :],
                          start=True, stop=True).then_inc(scores_done, 1)

            def values(t, kb, pair):
                c, h = pair // 2, 2 * pair
                pe.wait_ge(exp_done, t * H + h + 2)
                if pair % 2 == 0 and not (first(t) and c == 0):
                    pe.wait_ge(att_moved, t * C + c)
                if pair == 0 and not first(t):
                    pe.wait_ge(rden_done, t)
                rows = lambda n: slice(HD * (n % HC), HD * (n % HC + 1))
                for n in (h, h + 1):
                    pe.matmul(AT[rows(n), :], v_kv[kb][:, n * HD:(n + 1) * HD], prob[:, n % PR, :], start=True,
                              stop=True)
                for n in (h, h + 1):
                    ins = pe.matmul(DEN[rows(n + 2), :], den_sel[:, c, :], prob[:, n % PR, :], start=c == 0,
                                    stop=c == C - 1)
                ins.then_inc(pv_done, 1)

            def spread(T, c):
                if c == 0:
                    pe.wait_ge(rden_lo_done, T + 1)
                pe.matmul(spread_bank[c][:, :], bc_sel[:, c, :], rden_hi, start=True, stop=False)
                pe.matmul(spread_bank[c][:, :], bc_sel[:, c, :], rden_lo, start=False, stop=True).then_inc(spread_done, 1)

            def project_o(T, j):
                cols = slice(j * P, (j + 1) * P)
                if j == 0:
                    pe.wait_ge(at_lo_done, T * C + C)
                three_pass(o_bank[j][:, :], [(at_hi[:, c, cols], at_lo[:, c, cols], wo_hi[:, c, :], wo_lo[:, c, :])
                                             for c in range(C)]).then_inc(o_done, 1)

            def turn_z2(T, j):
                pe.wait_ge(z2_done, T * TB + j + 1)
                turn(z2_bank[j], columns(z2[:, j % 2, :]), z2_turned)

            def project_s(T):
                pe.wait_ge(z2t_lo_done, T * TB + TB)
                both = lambda w, c: w[:, c, :, :].rearrange("p a m -> p (a m)")
                three_pass(s_bank[:, :], [(both(win_hi, c), both(win_lo, c), z2t_hi[:, c, :], z2t_lo[:, c, :])
                                         for c in range(C)]).then_inc(s_mm_done, 1)

            def sum_hidden(T, hh):
                half = hh % 2
                if isinstance(T, int) and T == BLOCKS - 1:
                    pe.wait_ge(odd_hidden if half else hid_done, hh // 2 + 1 + (0 if half else T * HH))
                else:
                    pe.wait_ge(hid_done, T * HH + hh + 1)
                pe.matmul(g_bank[M * half:M * (half + 1), :], w2_diag[:, hh, :], hid[:, hh % RR, :],
                          start=hh < 2, stop=hh >= HH - 2).then_inc(hsum_done, 1)

            def project_y(T, j):
                if j == 0:
                    pe.wait_ge(g_done, T + 1)
                cols = slice(j * P, (j + 1) * P)
                three_pass(y_bank[j][:, :], [(g_hi[:, cols], g_lo[:, cols], wout_hi[:, :], wout_lo[:, :])]).then_inc(y_done, 1)

            def iteration(t, kb, kf, g, f, a, b):
                F, B, prologue = t + 1, t - 1, isinstance(t, int) and t == -1
                f_before = not isinstance(t, int) or 0 <= t < BLOCKS
                a_before = not isinstance(t, int) or 1 <= t <= BLOCKS
                b_before = not isinstance(t, int) or t >= 2
                if f:
                    last_user((f_before, mx_done[0], t * MAX_TILES + 4), (a_before, exp_done, (t - 1) * H + 16),
                              (b_before, z2t_lo_done, (t - 2) * TB + 3))
                    turn_z1(F, 0)
                    last_user((f_before, mx_done[0], t * MAX_TILES + 5), (a_before, exp_done, (t - 1) * H + 7),
                              (b_before, att_done, (t - 2) * C + 3))
                    turn_z1(F, 1)
                if prologue:
                    project_keys()
                if b:
                    last_user((f_before, mx_done[0], t * MAX_TILES + 6), (a_before, exp_done, (t - 1) * H + 14),
                              (b_before, z2t_lo_done, (t - 2) * TB + 1))
                    spread(B, 0)
                    last_user((f_before, mx_done[0], t * MAX_TILES + 7), (b_before, out_done, (t - 2) * TB + 3),
                              (a_before, exp_done, (t - 1) * H + 15))
                    spread(B, 1)
                if f:
                    last_user((f_before, mx_done[0], t * MAX_TILES + 8), (b_before, out_done, (t - 2) * TB + 4),
                              (a_before, exp_done, (t - 1) * H + 2))
                    turn_z1(F, 2)
                if a:
                    last_user((f_before, qf_done, t * TB + 3), (b_before, z2t_lo_done, (t - 2) * TB + 2),
                              (a_before, exp_done, (t - 1) * H + 10))
                    max_scores(t, kb, 2, 0)
                if f:
                    pe.wait_ge(zt_lo_done, F * TB + 1)
                    project_q(F, 0)
                if b:
                    last_user((f, zt_lo_done, F * TB + 2), (f_before, mx_done[0], t * MAX_TILES + 5),
                              (a_before, exp_done, (t - 1) * H + 7), (b_before, att_done, (t - 2) * C + 3))
                    spread(B, 2)
                    last_user((a, mx_done[1], t * MAX_TILES + 1), (f_before, qf_done, t * TB + 3),
                              (b_before, z2t_lo_done, (t - 2) * TB + 2), (a_before, exp_done, (t - 1) * H + 10))
                    spread(B, 3)
                if a:
                    last_user((b, att_done, B * C + 2), (f_before, mx_done[0], t * MAX_TILES + 7),
                              (b_before, out_done, (t - 2) * TB + 3), (a_before, exp_done, (t - 1) * H + 15))
                    max_scores(t, kb, 2, 1)
                if f:
                    last_user((b, att_done, B * C + 1), (f_before, mx_done[0], t * MAX_TILES + 6),
                              (a_before, exp_done, (t - 1) * H + 14), (b_before, z2t_lo_done, (t - 2) * TB + 1))
                    turn_z1(F, 3)
                    last_user((b, att_done, B * C + 3), (f, zt_lo_done, F * TB + 2))
                    project_q(F, 1)
                if a:
                    last_user((f, u_done, F * TB + 1), (f_before, mx_done[0], t * MAX_TILES + 4),
                              (a_before, exp_done, (t - 1) * H + 16), (b_before, z2t_lo_done, (t - 2) * TB + 3))
                    max_scores(t, kb, 2, 2)
                    last_user((b, att_done, B * C + 4), (a, mx_done[1], t * MAX_TILES + 1))
                    max_scores(t, kb, 2, 3)
                    last_user((f, zt_lo_done, F * TB + 3), (f_before, mx_done[0], t * MAX_TILES + 8),
                              (b_before, out_done, (t - 2) * TB + 4), (a_before, exp_done, (t - 1) * H + 2))
                    max_scores(t, kb, 3, 0)
                if f:
                    last_user((a, mx_done[1], t * MAX_TILES + 2), (b, att_done, B * C + 2),
                              (f_before, mx_done[0], t * MAX_TILES + 7), (b_before, out_done, (t - 2) * TB + 3),
                              (a_before, exp_done, (t - 1) * H + 15))
                    project_q(F, 2)
                if a:
                    last_user((f, zt_lo_done, F * TB + 4), (b, att_done, B * C + 1),
                              (f_before, mx_done[0], t * MAX_TILES + 6), (a_before, exp_done, (t - 1) * H + 14),
                              (b_before, z2t_lo_done, (t - 2) * TB + 1))
                    max_scores(t, kb, 3, 1)
                    pe.wait_ge(mx_done[1], t * MAX_TILES + 4)
                    max_scores(t, kb, 3, 2)
                    pe.wait_ge(mx_done[1], t * MAX_TILES + 3)
                    max_scores(t, kb, 3, 3)
                if b:
                    last_user((a, mx_done[1], t * MAX_TILES + 5), (f, zt_lo_done, F * TB + 3),
                              (f_before, mx_done[0], t * MAX_TILES + 8), (b_before, out_done, (t - 2) * TB + 4),
                              (a_before, exp_done, (t - 1) * H + 2))
                    project_o(B, 0)
                if f:
                    pe.wait_ge(u_done, F * TB + 2)
                    project_q(F, 3)
                if prologue:
                    turn_keys()
                    project_values()
                if a:
                    pe.wait_ge(mx_done[1], t * MAX_TILES + 7)
                    turn_max(t)
                if b:
                    last_user((a, mx_done[1], t * MAX_TILES + 8), (f, u_done, F * TB + 1),
                              (f_before, mx_done[0], t * MAX_TILES + 4), (a_before, exp_done, (t - 1) * H + 16),
                              (b_before, z2t_lo_done, (t - 2) * TB + 3))
                    project_o(B, 1)
                    last_user((f, u_done, F * TB + 3), (a, mx_done[1], t * MAX_TILES + 2), (b, att_done, B * C + 2))
                    project_o(B, 2)
                if a:
                    last_user((f, u_done, F * TB + 4), (b, att_done, B * C + 3),
                              (f_before, mx_done[0], t * MAX_TILES + 5), (a_before, exp_done, (t - 1) * H + 7))
                    scores(t, kb, 0)
                    last_user((b, x1_done, B * TB + 1), (a, mx_done[1], t * MAX_TILES + 5))
                    scores(t, kb, 1)
                    pe.wait_ge(mx_done[1], t * MAX_TILES + 6)
                    scores(t, kb, 2)
                if b:
                    pe.wait_ge(x1_done, B * TB + 2)
                    project_o(B, 3)
                if a:
                    last_user((b, x1_done, B * TB + 3), (f, u_done, F * TB + 3), (a, mx_done[1], t * MAX_TILES + 2))
                    scores(t, kb, 3)
                    values(t, kb, 0)
                    pe.wait_ge(exp_done, t * H + 3)
                    scores(t, kb, 4)
                    pe.wait_ge(mxt_done, t + 1)
                    scores(t, kb, 5)
                    values(t, kb, 1)
                    pe.wait_ge(exp_done, t * H + 1)
                    scores(t, kb, 6)
                    last_user((b, x1_done, B * TB + 4), (a, mx_done[1], t * MAX_TILES + 8))
                    scores(t, kb, 7)
                    pe.wait_ge(exp_done, t * H + 5)
                    scores(t, kb, 8)
                if f:
                    last_user((a, exp_done, t * H + 2), (b, x1_done, B * TB + 1), (f, zt_lo_done, F * TB + 3))
                    turn_q(F, 0)
                if a:
                    pe.wait_ge(exp_done, t * H + 6)
                    scores(t, kb, 9)
                    values(t, kb, 2)
                    values(t, kb, 3)
                    pe.wait_ge(exp_done, t * H + 8)
                    scores(t, kb, 10)
                    pe.wait_ge(exp_done, t * H + 4)
                    scores(t, kb, 11)
                if b:
                    last_user((a, exp_done, t * H + 9), (f, zt_lo_done, F * TB + 4), (b, att_done, B * C + 1))
                    turn_z2(B, 0)
                    last_user((a, exp_done, t * H + 10), (b, att_done, B * C + 4))
                    turn_z2(B, 1)
                if f:
                    last_user((a, exp_done, t * H + 7), (f, u_done, F * TB + 4))
                    turn_q(F, 1)
                if a:
                    values(t, kb, 4)
                if b:
                    last_user((a, exp_done, t * H + 11), (b, x1_done, B * TB + 4))
                    turn_z2(B, 2)
                    last_user((f, qf_done, F * TB + 1), (a, exp_done, t * H + 2), (b, x1_done, B * TB + 1))
                    turn_z2(B, 3)
                if a:
                    pe.wait_ge(exp_done, t * H + 12)
                    scores(t, kb, 12)
                    last_user((b, z2t_lo_done, B * TB + 1), (a, exp_done, t * H + 9))
                    scores(t, kb, 13)
                    values(t, kb, 5)
                if f:
                    last_user((b, z2t_lo_done, B * TB + 2), (a, exp_done, t * H + 10), (f_before, qf_done, t * TB + 3))
                    turn_q(F, 2)
                if a:
                    pe.wait_ge(exp_done, t * H + 13)
                    scores(t, kb, 14)
                    last_user((b, z2t_lo_done, B * TB + 3), (a, exp_done, t * H + 11))
                    scores(t, kb, 15)
                if b:
                    pe.wait_ge(z2t_lo_done, B * TB + 4)
                    project_s(B)
                if f:
                    last_user((a, exp_done, t * H + 14), (b, z2t_lo_done, B * TB + 1), (f, zt_lo_done, F * TB + 4))
                    max_scores(F, kf, 0, 0)
                if a:
                    values(t, kb, 6)
                if f:
                    last_user((b, s_done, B + 1), (f, qf_done, F * TB + 1))
                    max_scores(F, kf, 0, 1)
                    last_user((a, exp_done, t * H + 15), (b, x1_done, B * TB + 3), (f, u_done, F * TB + 3))
                    max_scores(F, kf, 0, 2)
                if a:
                    values(t, kb, 7)
                if b:
                    last_user((f, mx_done[0], F * MAX_TILES + 2), (b, s_done, B + 1))
                    sum_hidden(B, 0)
                if f:
                    pe.wait_ge(mx_done[0], F * MAX_TILES + 1)
                    turn_q(F, 3)
                if b:
                    sum_hidden(B, 1)
                    sum_hidden(B, 2)
                    sum_hidden(B, 3)
                    sum_hidden(B, 4)
                    sum_hidden(B, 5)
                    sum_hidden(B, 6)
                    sum_hidden(B, 7)
                if f:
                    last_user((a, exp_done, t * H + 16), (b, z2t_lo_done, B * TB + 3), (f, u_done, F * TB + 1))
                    max_scores(F, kf, 0, 3)
                    pe.wait_ge(qf_done, F * TB + 2)
                    max_scores(F, kf, 1, 0)
                    pe.wait_ge(qf_done, F * TB + 4)
                    max_scores(F, kf, 1, 1)
                if b:
                    last_user((f, mx_done[0], F * MAX_TILES + 3), (a, exp_done, t * H + 15), (b, x1_done, B * TB + 3))
                    project_y(B, 0)
                    pe.wait_ge(g_done, B + 1)
                    project_y(B, 1)
                    pe.wait_ge(out_done, B * TB + 1)
                    project_y(B, 2)
                    pe.wait_ge(out_done, B * TB + 2)
                    project_y(B, 3)
                if f:
                    last_user((b, out_done, B * TB + 3), (f, mx_done[0], F * MAX_TILES + 3))
                    max_scores(F, kf, 1, 2)
                    last_user((b, out_done, B * TB + 4), (f, mx_done[0], F * MAX_TILES + 2))
                    max_scores(F, kf, 1, 3)

            def enter():
                pe.wait_ge(weights_split, WEIGHTS)
                pe.wait_ge(keys_stacked, 16 * NB * G * 3)
                pe.wait_ge(params_loaded, PARAMS)

            def last(B):
                t = B + 1
                pe.wait_ge(exp_done, (t - 1) * H + 14)
                spread(B, 0)
                pe.wait_ge(out_done, (t - 2) * TB + 3)
                spread(B, 1)
                pe.wait_ge(exp_done, (t - 1) * H + 7)
                spread(B, 2)
                pe.wait_ge(z2t_lo_done, (t - 2) * TB + 2)
                spread(B, 3)
                pe.wait_ge(out_done, (t - 2) * TB + 4)
                project_o(B, 0)
                pe.wait_ge(exp_done, (t - 1) * H + 16)
                project_o(B, 1)
                pe.wait_ge(att_done, B * C + 2)
                project_o(B, 2)
                pe.wait_ge(x1_done, B * TB + 2)
                project_o(B, 3)
                pe.wait_ge(att_done, B * C + 1)
                turn_z2(B, 0)
                pe.wait_ge(att_done, B * C + 4)
                turn_z2(B, 1)
                pe.wait_ge(x1_done, B * TB + 4)
                turn_z2(B, 2)
                pe.wait_ge(x1_done, B * TB + 1)
                turn_z2(B, 3)
                pe.wait_ge(z2t_lo_done, B * TB + 4)
                project_s(B)
                pe.wait_ge(s_done, B + 1)
                sum_hidden(B, 0)
                sum_hidden(B, 1)
                sum_hidden(B, 2)
                sum_hidden(B, 3)
                sum_hidden(B, 4)
                sum_hidden(B, 5)
                sum_hidden(B, 6)
                sum_hidden(B, 7)
                pe.wait_ge(x1_done, B * TB + 3)
                project_y(B, 0)
                pe.wait_ge(g_done, B + 1)
                project_y(B, 1)
                pe.wait_ge(out_done, B * TB + 1)
                project_y(B, 2)
                pe.wait_ge(out_done, B * TB + 2)
                project_y(B, 3)

            iterations(pe, iteration, last, enter)


_INS = ['x', 'ctx_1024', 'L0_xattn_Wq', 'L0_xattn_Wk', 'L0_xattn_Wv', 'L0_xattn_Wo', 'L0_xattn_gq', 'L0_xattn_bq',
        'L0_xattn_gk', 'L0_xattn_bk', 'L0_ffn_Win', 'L0_ffn_bin_', 'L0_ffn_W1', 'L0_ffn_b1', 'L0_ffn_W2',
        'L0_ffn_b2', 'L0_ffn_Wout', 'L0_ffn_bout']


def kernel(**inputs):
    import numpy as _np
    import concourse.bacc as _bacc
    from concourse import mybir as _mybir
    from concourse.bass_utils import run_bass_kernel_spmd as _run

    nc = _bacc.Bacc("TRN2", target_bir_lowering=False, num_devices=1)
    arrays, args = {}, []
    for name in _INS:
        a = _np.ascontiguousarray(inputs[name])
        arrays[f"in_{name}_dram"] = a
        args.append(nc.dram_tensor(f"in_{name}_dram", a.shape, _mybir.dt.from_np(a.dtype), kind="ExternalInput").ap())
    args.append(nc.dram_tensor("out_0_dram", inputs['x'].shape, _mybir.dt.float32, kind="ExternalOutput").ap())
    build_program(nc, *args)
    r = _run(nc, [arrays], core_ids=[0])
    return r.results[0]["out_0_dram"]
```
